# Optimizing a Trainium2 kernel written in Bass

```python
import numpy as np
import jax
import jax.numpy as jnp

def _softmax(x, axis=-1):
    return jax.nn.softmax(x, axis=axis)

def _gelu(x):
    return jax.nn.gelu(x, approximate=True)

def _silu(x):
    return jax.nn.silu(x)

def _sigmoid(x):
    return jax.nn.sigmoid(x)

def _layernorm(x, axis=-1, eps=1e-05):
    m = jnp.mean(x, axis=axis, keepdims=True)
    v = jnp.var(x, axis=axis, keepdims=True)
    return (x - m) / jnp.sqrt(v + eps)

def _scatter_add(tgt, idx, src, axis=0):
    return tgt.at[idx].add(src)

def _segment_sum(src, seg, n):
    return jax.ops.segment_sum(src, seg, n)
kernel_name = 'mk_flamingo_gated_d1_seqx_r8_05314f'

def setup_inputs(seed: int=0):
    np.random.seed(seed)
    _w = jnp.asarray

    def _rec_inputs():
        import jax
        import jax.numpy as jnp
        _rk = jax.random.key(seed)
        x = -0.0002928 + 1 * jax.random.normal(jax.random.fold_in(_rk, 1), (8, 56, 128), jnp.float32)
        _lenS = 56 - jax.random.randint(jax.random.fold_in(_rk, 7), (8,), 0, max(1, 56 // 4) + 1, jnp.int32)
        _lenS2 = 1500 - jax.random.randint(jax.random.fold_in(_rk, 8), (8,), 0, max(1, 1500 // 4) + 1, jnp.int32)
        _ctx_1024P = jax.random.normal(jax.random.fold_in(_rk, 11), (8, 16, 128), jnp.float32)
        _ctx_1024c = jax.random.dirichlet(jax.random.fold_in(_rk, 511), 0.3 * jnp.ones((16,), jnp.float32), (8, 1500))
        _ctx_1024t = jnp.einsum('bsk,bkd->bsd', _ctx_1024c, _ctx_1024P)
        _ctx_1024t = _ctx_1024t * jax.lax.rsqrt(jnp.mean(jnp.square(_ctx_1024t)) + 1e-12) * 0.953939
        ctx_1024 = -1.39393e-06 + 0.999914 * (_ctx_1024t + 0.3 * jax.random.normal(jax.random.fold_in(_rk, 611), (8, 1500, 128), jnp.float32))
        _g = jax.random.normal(jax.random.fold_in(_rk, 9001), (2, 1), jnp.float32)
        _g = jnp.sign(_g) * jnp.maximum(jnp.abs(_g), 1.0) + (_g == 0) * 1.0
        g_xattn = _g[0]
        g_ffn = _g[1]
        return (x, ctx_1024, g_xattn, g_ffn)
    x, ctx_1024, g_xattn, g_ffn = _rec_inputs()

    def _L0_xattn_setup():
        import jax, jax.numpy as jnp
        import numpy as np
        HIDDEN, HEADS, HEAD_DIM = (128, 16, 64)
        BSZ, SEQ = (2, 256)
        SCALE = HEAD_DIM ** (-0.5)
        CAUSAL = True
        key = jax.random.key(seed)
        ks = jax.random.split(key, 7)
        inner = HEADS * HEAD_DIM
        init = lambda k, shape: jax.random.normal(k, shape, dtype=jnp.float32) * shape[0] ** (-0.5)
        return {'query': jax.random.normal(ks[0], (BSZ, SEQ, HIDDEN), dtype=jnp.float32), 'key': jax.random.normal(ks[1], (BSZ, SEQ, HIDDEN), dtype=jnp.float32), 'value': jax.random.normal(ks[2], (BSZ, SEQ, HIDDEN), dtype=jnp.float32), 'w_q': init(ks[3], (HIDDEN, inner)), 'w_k': init(ks[4], (HIDDEN, inner)), 'w_v': init(ks[5], (HIDDEN, inner)), 'w_o': init(ks[6], (inner, HIDDEN))}
    _L0_xattn_all = _L0_xattn_setup()
    _L0_xattn_in = {k: v for k, v in _L0_xattn_all.items() if k in ('w_q', 'w_k', 'w_v', 'w_o')}
    del _L0_xattn_all

    def _L0_ffn_setup():
        import jax, jax.numpy as jnp
        import numpy as np
        D_MODEL = 128
        HIDDEN = 256
        E_ROUTED = 14
        E_SHARED = 2
        TOP_K = 2
        EPS = 1e-09
        RMS_EPS = 1.1920929e-07

        def _ffn(xn, rw, W1, W2):
            ms = jnp.mean(xn * xn, axis=-1, keepdims=True)
            h = xn * jax.lax.rsqrt(ms + RMS_EPS) * rw
            return jax.nn.silu(h @ W1) @ W2
        key = jax.random.key(seed)
        ks = jax.random.split(key, 9)
        B, T = (2, 128)
        x = jax.random.normal(ks[0], (B, T, D_MODEL), dtype=jnp.float32)
        router_w = jax.random.normal(ks[1], (D_MODEL, E_ROUTED), dtype=jnp.float32) * 0.006
        rms_w = jnp.ones((E_ROUTED, D_MODEL), dtype=jnp.float32)
        w1 = jax.random.normal(ks[2], (E_ROUTED, D_MODEL, HIDDEN), dtype=jnp.float32) * 0.02
        w2 = jax.random.normal(ks[3], (E_ROUTED, HIDDEN, D_MODEL), dtype=jnp.float32) * 0.02
        rms_w_s = jnp.ones((E_SHARED, D_MODEL), dtype=jnp.float32)
        w1_s = jax.random.normal(ks[4], (E_SHARED, D_MODEL, HIDDEN), dtype=jnp.float32) * 0.02
        w2_s = jax.random.normal(ks[5], (E_SHARED, HIDDEN, D_MODEL), dtype=jnp.float32) * 0.02
        return {'x': x, 'router_w': router_w, 'rms_w': rms_w, 'w1': w1, 'w2': w2, 'rms_w_s': rms_w_s, 'w1_s': w1_s, 'w2_s': w2_s}
    _L0_ffn_all = _L0_ffn_setup()
    _L0_ffn_in = {k: v for k, v in _L0_ffn_all.items() if k in ('router_w', 'rms_w', 'w1', 'w2', 'rms_w_s', 'w1_s', 'w2_s')}
    del _L0_ffn_all
    return {'x': x, 'ctx_1024': ctx_1024, 'g_xattn': g_xattn, 'g_ffn': g_ffn, 'L0_xattn_w_q': _L0_xattn_in['w_q'], 'L0_xattn_w_k': _L0_xattn_in['w_k'], 'L0_xattn_w_v': _L0_xattn_in['w_v'], 'L0_xattn_w_o': _L0_xattn_in['w_o'], 'L0_ffn_router_w': _L0_ffn_in['router_w'], 'L0_ffn_rms_w': _L0_ffn_in['rms_w'], 'L0_ffn_w1': _L0_ffn_in['w1'], 'L0_ffn_w2': _L0_ffn_in['w2'], 'L0_ffn_rms_w_s': _L0_ffn_in['rms_w_s'], 'L0_ffn_w1_s': _L0_ffn_in['w1_s'], 'L0_ffn_w2_s': _L0_ffn_in['w2_s']}

def reference(x, ctx_1024, g_xattn, g_ffn, L0_xattn_w_q, L0_xattn_w_k, L0_xattn_w_v, L0_xattn_w_o, L0_ffn_router_w, L0_ffn_rms_w, L0_ffn_w1, L0_ffn_w2, L0_ffn_rms_w_s, L0_ffn_w1_s, L0_ffn_w2_s):
    import jax
    import jax.numpy as jnp

    def _L0_xattn_ref(query, key, value, w_q, w_k, w_v, w_o):
        import jax, jax.numpy as jnp
        import numpy as np
        HIDDEN, HEADS, HEAD_DIM = (128, 16, 64)
        BSZ, SEQ = (2, 256)
        SCALE = HEAD_DIM ** (-0.5)
        CAUSAL = True
        bsz, q_len, _ = query.shape
        k_len = key.shape[1]

        def split_heads(x):
            return x.reshape(x.shape[0], x.shape[1], HEADS, HEAD_DIM).transpose(0, 2, 1, 3)
        q = split_heads(query @ w_q)
        k = split_heads(key @ w_k)
        v = split_heads(value @ w_v)
        scores = jnp.einsum('bhqd,bhkd->bhqk', q, k) * SCALE
        if CAUSAL:
            q_pos = jnp.arange(q_len)
            k_pos = jnp.arange(k_len)
            mask = (k_pos[None, :] <= q_pos[:, None]).astype(scores.dtype)
            scores = scores + (1.0 - mask)[None, None, :, :] * -10000.0
        weights = jax.nn.softmax(scores, axis=-1)
        out = jnp.einsum('bhqk,bhkd->bhqd', weights, v)
        out = out.transpose(0, 2, 1, 3).reshape(bsz, q_len, HEADS * HEAD_DIM)
        return out @ w_o

    def _L0_ffn_ref(x, router_w, rms_w, w1, w2, rms_w_s, w1_s, w2_s):
        import jax, jax.numpy as jnp
        import numpy as np
        D_MODEL = 128
        HIDDEN = 256
        E_ROUTED = 14
        E_SHARED = 2
        TOP_K = 2
        EPS = 1e-09
        RMS_EPS = 1.1920929e-07

        def _ffn(xn, rw, W1, W2):
            ms = jnp.mean(xn * xn, axis=-1, keepdims=True)
            h = xn * jax.lax.rsqrt(ms + RMS_EPS) * rw
            return jax.nn.silu(h @ W1) @ W2
        B, T, D = x.shape
        N = B * T
        xf = x.reshape(N, D)
        gates = jax.nn.softmax(xf @ router_w, axis=-1)
        top_v, top_i = jax.lax.top_k(gates, TOP_K)
        masked = jnp.zeros_like(gates).at[jnp.arange(N)[:, None], top_i].set(top_v)
        masked = masked / (masked.sum(axis=-1, keepdims=True) + EPS)
        routed = jax.vmap(lambda rw_, W1_, W2_: _ffn(xf, rw_, W1_, W2_))(rms_w, w1, w2)
        routed_out = jnp.einsum('end,ne->nd', routed, masked)
        shared = jax.vmap(lambda rw_, W1_, W2_: _ffn(xf, rw_, W1_, W2_))(rms_w_s, w1_s, w2_s).sum(0)
        return (routed_out + shared).reshape(B, T, D)
    x = x + jnp.tanh(g_xattn[0]) * _L0_xattn_ref(_layernorm(x, axis=-1), ctx_1024, ctx_1024, L0_xattn_w_q, L0_xattn_w_k, L0_xattn_w_v, L0_xattn_w_o)
    x = x + jnp.tanh(g_ffn[0]) * _L0_ffn_ref(_layernorm(x, axis=-1), L0_ffn_router_w, L0_ffn_rms_w, L0_ffn_w1, L0_ffn_w2, L0_ffn_rms_w_s, L0_ffn_w1_s, L0_ffn_w2_s)
    return x

_drawn_inputs = setup_inputs


def setup_inputs(seed=0):
    import zlib

    import numpy as np

    out = dict(_drawn_inputs(seed))
    spreads = {'L0_ffn_rms_w': (1.0, 0.6), 'L0_ffn_rms_w_s': (1.0, 0.6)}
    factors = {}
    for name, (base, spread) in spreads.items():
        noise = np.random.default_rng([zlib.crc32(name.encode()), seed]).standard_normal(out[name].shape)
        drawn = base * np.exp(spread * noise) if base else spread * noise
        out[name] = jnp.asarray(drawn.astype(out[name].dtype))
    for name, factor in factors.items():
        out[name] = (out[name] * factor).astype(out[name].dtype)
    return out
```

```python
from contextlib import ExitStack

import concourse.bass as bass
from concourse import mybir

FP32 = mybir.dt.float32
INT32 = mybir.dt.int32
ACT = mybir.ActivationFunctionType
ALU = mybir.AluOpType
AX = mybir.AxisListType

B, Q, D = 8, 56, 128
KEYS = 1500
HEADS, HEAD = 16, 64
INNER = HEADS * HEAD
ROUTED, SHARED, HIDDEN = 14, 2, 256
EXPERTS = ROUTED + SHARED
TOKENS = B * Q
P = 128
PAIRS = B // 2
ROWS = 2 * Q
SLOT = 64
BANK = 512
KC = 12
KP = KEYS // KC
CHUNKS = INNER // P
GROUPS = HEADS // 4

SCALE = HEAD ** -0.5
MASKED = -10000.0
LN_EPS = 1e-5
RMS_EPS = 1.1920929e-07
GATE_EPS = 1e-9

SCORE_LIMIT = 4900.0
GUARD_LIMIT = SCORE_LIMIT ** 2 / (SCALE ** 2 * D * P)


def head_of(group, i):
    return 8 * (group // 2) + 2 * i + group % 2


RING_JOBS = (
    ["wkT0", "wkT1", "wqT0", "wqT1", "ctxT"]
    + [f"A{g}" for g in range(GROUPS)]
    + [f"K{s}" for s in range(4)] + ["xnT"] + [f"K{s}" for s in range(4, HEADS)]
    + ["wvT0", "wvT1"] + [f"M{g}" for g in range(GROUPS)]
)
for _t in range(PAIRS):
    RING_JOBS += [f"P{_t}.{g}" for g in range(GROUPS)]
    RING_JOBS += [f"C{_t}.{bb}.{half}" for half in range(2) for bb in range(2)]
RING_BANKS = 4
LOOP_FROM = 3
LOOP_STEPS = (EXPERTS - LOOP_FROM - 1) // 4
G_HEAD_STEPS = 4
G_BATCH_STEPS = 1 + HEADS * G_HEAD_STEPS
ACT_JOBS = [j for n, j in enumerate(RING_JOBS) if j[0] in "PC" or (n % 2 == 0 and j != "xnT")]
DVE_JOBS = [j for j in RING_JOBS if j not in ACT_JOBS]


def build(nc, A, out):
    ctx = ExitStack()
    with ctx:
        def sb(name, shape, dt=FP32):
            return ctx.enter_context(nc.sbuf_tensor(name, shape, dt))

        def pb(name, shape, dt=FP32):
            return ctx.enter_context(nc.psum_tensor(name, shape, dt))

        def sem(name):
            return ctx.enter_context(nc.semaphore(name))

        wq = sb("wq", [P, INNER])
        wk = sb("wk", [P, INNER])
        wv = sb("wv", [P, INNER])
        wo = sb("wo", [P, CHUNKS, D])
        wqT = sb("wqT", [P, CHUNKS, D])
        wkT = sb("wkT", [P, CHUNKS, D])
        wvT = wkT
        A_T = sb("A_T", [P, HEADS, D])
        M = sb("M", [P, HEADS, D])
        x_rows = sb("x_rows", [ROWS, PAIRS, D])
        xn_rows = sb("xn_rows", [ROWS, PAIRS, D])
        xnT = sb("xnT", [P, B, SLOT])
        ctx_head = sb("ctx_head", [Q, B, D])
        ctx_headT = sb("ctx_headT", [P, B * Q])
        ctx_all = sb("ctx_all", [KP, B, KC * D])
        keyproj = sb("keyproj", [P, HEADS, B * Q])
        probs = sb("probs", [P, 2, HEADS, Q])
        probsT = sb("probsT", [Q, HEADS, ROWS])
        mixT = sb("mixT", [P, HEADS, ROWS])
        hidden_slots = sb("hidden_slots", [P, 2, 2, TOKENS])
        hidden = [hidden_slots[:, s, :, :] for s in range(2)]
        square_junk = hidden_slots[:, :, :, :].rearrange("p s c n -> p (s c n)")
        ident = sb("ident", [P, P])
        causal = sb("causal", [P, Q])
        causal_all = sb("causal_all", [Q, KC, 5])
        row_max = sb("row_max", [P, HEADS])
        row_sum = sb("row_sum", [P, HEADS])
        row_inv = sb("row_inv", [P, HEADS])
        ln_stats = sb("ln_stats", [ROWS, PAIRS, 6])
        ln_mv = sb("ln_mv", [ROWS, PAIRS, 2])
        ln_var = sb("ln_var", [ROWS, PAIRS])
        ln_rstd = sb("ln_rstd", [ROWS, PAIRS])
        minus_half = sb("minus_half", [ROWS, PAIRS])
        gate_col = sb("gate_col", [P, 2])
        tanh_col = sb("tanh_col", [P, 2])
        guard_parts = sb("guard_parts", [P, GROUPS + B])
        guard_max = sb("guard_max", [P, 2])
        guard_pair = sb("guard_pair", [1, 2])
        guard_prod = sb("guard_prod", [1, 1])
        guard_ok = sb("guard_ok", [1, 1], INT32)
        x1 = sb("x1", [ROWS, PAIRS, D])
        router_w = sb("router_w", [P, ROUTED])
        rms_rows = sb("rms_rows", [EXPERTS, D])
        rms_cols = sb("rms_cols", [P, EXPERTS])
        w1 = sb("w1", [P, EXPERTS, HIDDEN])
        w2 = sb("w2", [P, EXPERTS, 2, D])
        w1_scaled = [sb(f"w1_scaled{s}", [P, HIDDEN]) for s in range(2)]
        pow_base = sb("pow_base", [ROWS, 3, PAIRS])
        pow_exp = sb("pow_exp", [ROWS, 3, PAIRS])
        pow_out = sb("pow_out", [ROWS, 3, PAIRS])
        ratio = sb("ratio", [ROWS, PAIRS])
        h_rows = sb("h_rows", [ROWS, PAIRS, D])
        hT = sb("hT", [P, TOKENS])
        logits = sb("logits", [ROWS, PAIRS, ROUTED])
        shifted = sb("shifted", [ROWS, PAIRS, ROUTED])
        expo = sb("expo", [ROWS, PAIRS, ROUTED])
        rank = sb("rank", [ROWS, PAIRS, ROUTED])
        hit = [sb(f"hit{i}", [ROWS, PAIRS, ROUTED]) for i in range(2)]
        tie = [sb(f"tie{i}", [ROWS, PAIRS, ROUTED]) for i in range(2)]
        pick = [sb(f"pick{i}", [ROWS, PAIRS, ROUTED]) for i in range(2)]
        rest = sb("rest", [ROWS, PAIRS, ROUTED])
        chosen = sb("chosen", [ROWS, PAIRS, ROUTED])
        top = [sb(f"top{i}", [ROWS, PAIRS]) for i in range(2)]
        best_rank = [sb(f"best_rank{i}", [ROWS, PAIRS]) for i in range(2)]
        logit_max = sb("logit_max", [ROWS, PAIRS])
        exp_sum = sb("exp_sum", [ROWS, PAIRS])
        top_sum = sb("top_sum", [ROWS, PAIRS])
        gate_den = sb("gate_den", [ROWS, PAIRS])
        gate_inv = sb("gate_inv", [ROWS, PAIRS])
        gates = sb("gates", [ROWS, EXPERTS, PAIRS])
        moe = sb("moe", [ROWS, PAIRS, D])
        result = sb("result", [ROWS, PAIRS, D])

        def lay(space, at, rows, n):
            return space[0:rows, at:at + n]

        key_space = keyproj[:, :, :].rearrange("p h n -> p (h n)")
        prob_space = probs[:, :, :, :].rearrange("p s h k -> p (s h k)")
        mix_space = mixT[:, :, :].rearrange("p h n -> p (h n)")
        g_ctx = lay(key_space, 0, KP, KC * D).rearrange("p (c d) -> p c d", c=KC)
        g_ctxT = lay(key_space, 1536, P, KEYS)
        g_key = lay(key_space, 3072, P, KEYS)
        g_prob = lay(key_space, 4608, Q, KEYS)
        g_probT = lay(key_space, 6144, KP, KC * Q).rearrange("p (c q) -> p c q", c=KC)
        g_xnT = lay(prob_space, 0, P, Q)
        g_AT = lay(prob_space, 128, P, D)
        g_mixT = lay(prob_space, 256, P, Q)
        g_acc = lay(prob_space, 384, Q, D)
        attn_all = lay(mix_space, 0, ROWS, PAIRS * D).rearrange("p (t d) -> p t d", t=PAIRS)
        g_max = sb("g_max", [Q, 1])
        g_sum = sb("g_sum", [Q, 1])
        g_inv = sb("g_inv", [Q, 1])
        g_attn_dram = nc.dram_tensor("g_attn_dram", [TOKENS, D], FP32, kind="Internal").ap()

        ring = pb("ring", [P, RING_BANKS, BANK])
        score_ps = pb("score_ps", [P, 2, BANK])
        attn_ps = pb("attn_ps", [P, BANK])
        misc_ps = pb("misc_ps", [P, BANK])

        names = """wk_loaded wq_loaded wv_loaded wo_loaded x_loaded ctx_head_loaded gates_loaded
            router_loaded rms_loaded w1_loaded w2_loaded
            ident_zero ident_ready causal_zero causal_slots causal_ready slots_zero moe_consts_ready
            ring_filled act_drained dve_drained vector_steps
            ln1_var_ready ln1_rstd_ready xn_ready tanh_ready
            scores_ready scores_read shifted_ready exp_ready probs_ready attn_done x1_ready
            squares_done guard_max_ready guard_rows_ready guard_ready
            pow_base_ready pow_ready h_ready hT_filled hT_ready rms_filled rms_ready
            logits_filled logits_ready router_exp_ready
            w1_scaled_ready hidden_filled hidden_ready expert_done acc_done result_ready stored
            g_batch_ready g_ctxT_filled g_ctxT_ready g_A_ready
            g_key_filled g_key_ready g_score_filled g_max_ready g_exp_ready g_prob_ready
            g_probT_filled g_probT_ready g_mix_filled g_mix_ready g_out_filled g_vector_steps
            g_stored g_loaded g_x1_ready""".split()
        S = {n: sem(n) for n in names}
        ctx_loaded = [sem(f"ctx_loaded{b}") for b in range(B)]

        def bank_of(job):
            return RING_JOBS.index(job) % RING_BANKS

        def evacuated(job):
            if job in ACT_JOBS:
                return S["act_drained"], ACT_JOBS.index(job) + 1
            return S["dve_drained"], DVE_JOBS.index(job) + 1

        def wait_bank_free(pe, job):
            n = RING_JOBS.index(job)
            if n >= RING_BANKS:
                pe.wait_ge(*evacuated(RING_JOBS[n - RING_BANKS]))

        def wait_filled(eng, job):
            eng.wait_ge(S["ring_filled"], RING_JOBS.index(job) + 1)

        def bank(job, cols=BANK, rows=P):
            return ring[0:rows, bank_of(job), 0:cols]

        def evacuation(job):
            kind = job.rstrip("0123456789.")
            if kind in ("wkT", "wqT", "wvT"):
                dst = {"wkT": wkT, "wqT": wqT, "wvT": wvT}[kind]
                n = int(job[3:])
                return dst[:, 4 * n:4 * n + 4, :], bank(job).rearrange("p (c d) -> p c d", c=4)
            if kind == "ctxT":
                return ctx_headT[:, :], bank(job, B * Q)
            if kind == "xnT":
                return xnT[:, :, 0:Q], bank(job, TOKENS).rearrange("p (b q) -> p b q", b=B)
            if kind in "AM":
                g = int(job[1:])
                dst = {"A": A_T, "M": M}[kind]
                return dst[:, 4 * g:4 * g + 4, :], bank(job).rearrange("p (c d) -> p c d", c=4)
            if kind == "K":
                return keyproj[:, int(job[1:]), :], bank(job, B * Q)
            if kind == "P":
                g = int(job.split(".")[1])
                src = bank(job, rows=Q).rearrange("p (h b s) -> p h b s", h=4, b=2)[:, :, :, 0:Q]
                return probsT[:, 4 * g:4 * g + 4, :].rearrange("p h (b q) -> p h b q", b=2), src
            bb, half = int(job.split(".")[1]), int(job.split(".")[2])
            return (mixT[:, 8 * half:8 * half + 8, bb * Q:bb * Q + Q],
                    bank(job, 8 * Q).rearrange("p (h q) -> p h q", h=8))

        block = ctx.enter_context(nc.Block())

        @block.sync
        def _(sp):
            sp.dma_start(wk[:, :], A["L0_xattn_w_k"]).then_inc(S["wk_loaded"], 16)
            sp.dma_start(wq[:, :], A["L0_xattn_w_q"]).then_inc(S["wq_loaded"], 16)
            sp.dma_start(wv[:, :], A["L0_xattn_w_v"]).then_inc(S["wv_loaded"], 16)
            sp.dma_start(wo[:, :, :], A["L0_xattn_w_o"].rearrange("(c p) n -> p c n", p=P))\
                .then_inc(S["wo_loaded"], 16)
            for b in range(B):
                sp.dma_start(ctx_all[:, b, :],
                             A["ctx_1024"][b, :, :].rearrange("(p c) d -> p (c d)", c=KC))\
                    .then_inc(ctx_loaded[b], 16)
            sp.dma_start(w1[:, 0:SHARED, :], A["L0_ffn_w1_s"].rearrange("e p f -> p e f"))\
                .then_inc(S["w1_loaded"], 16)
            sp.dma_start(w2[:, 0:SHARED, :, :],
                         A["L0_ffn_w2_s"].rearrange("e (c p) n -> p e c n", p=P))\
                .then_inc(S["w2_loaded"], 16)
            sp.dma_start(w1[:, SHARED:EXPERTS, :], A["L0_ffn_w1"].rearrange("e p f -> p e f"))\
                .then_inc(S["w1_loaded"], 16)
            sp.dma_start(w2[:, SHARED:EXPERTS, :, :],
                         A["L0_ffn_w2"].rearrange("e (c p) n -> p e c n", p=P))\
                .then_inc(S["w2_loaded"], 16)
            out_rows = out.rearrange("b q d -> (b q) d").rearrange("(t p) d -> p t d", p=ROWS)
            for t in range(PAIRS):
                sp.wait_ge(S["result_ready"], t + 1)
                sp.dma_start(out_rows[:, t, :], result[:, t, :]).then_inc(S["stored"], 16)
            sp.wait_ge(S["stored"], 16 * PAIRS)

        @block.gpsimd
        def _(pool):
            nc.gpsimd.memset(ident[:, :], 0.0).then_inc(S["ident_zero"], 1)
            nc.gpsimd.memset(minus_half[:, :], -0.5)
            pool.wait_ge(S["ident_zero"], 1)
            nc.gpsimd.affine_select(out=ident[:, :], in_=ident[:, :], compare_op=ALU.not_equal,
                                    fill=1.0, base=0, pattern=[[-1, P]], channel_multiplier=1)\
                .then_inc(S["ident_ready"], 1)
            nc.gpsimd.memset(xnT[:, :, :], 0.0).then_inc(S["slots_zero"], 1)
            nc.gpsimd.memset(causal[:, :], 0.0)
            nc.gpsimd.memset(causal_all[:, :, :], 0.0)
            nc.gpsimd.memset(guard_parts[:, :], 0.0).then_inc(S["causal_zero"], 1)
            pool.wait_ge(S["causal_zero"], 1)
            pool.wait_ge(S["ln1_var_ready"], 1)
            nc.gpsimd.tensor_tensor(ln_rstd[:, :], ln_var[:, :], minus_half[:, :], ALU.pow)\
                .then_inc(S["ln1_rstd_ready"], 1)
            pool.wait_ge(S["ln1_rstd_ready"], 1)
            for s in range(2):
                rows = causal[s * SLOT:(s + 1) * SLOT, :]
                nc.gpsimd.affine_select(out=rows, in_=rows, compare_op=ALU.is_ge, fill=MASKED,
                                        base=0, pattern=[[-1, Q]], channel_multiplier=1)\
                    .then_inc(S["causal_slots"], 1)
                pool.wait_ge(S["causal_slots"], s + 1)
            nc.gpsimd.affine_select(out=causal_all[:, :, :], in_=causal_all[:, :, :],
                                    compare_op=ALU.is_ge, fill=MASKED, base=0,
                                    pattern=[[-1, KC], [-KC, 5]], channel_multiplier=1)\
                .then_inc(S["causal_ready"], 1)
            nc.gpsimd.iota(rank[:, :, :], pattern=[[0, PAIRS], [-1, ROUTED]], base=ROUTED,
                           channel_multiplier=0, allow_small_or_imprecise_dtypes=True)
            nc.gpsimd.memset(pow_exp[:, 0, :], -0.5)
            nc.gpsimd.memset(pow_exp[:, 1, :], 0.5)
            nc.gpsimd.memset(pow_exp[:, 2, :], -0.5)
            nc.gpsimd.memset(gates[:, 0:SHARED, :], 1.0).then_inc(S["moe_consts_ready"], 1)

            def scale_w1(e, slot):
                nc.gpsimd.tensor_scalar(w1_scaled[slot][:, :], w1[:, e, :], rms_col(e), None,
                                        ALU.mult).then_inc(S["w1_scaled_ready"], 1)

            def rms_col(e):
                return rms_cols[:, bass.ds(e, 1)]

            def scale_w1(e):
                nc.gpsimd.tensor_tensor(w1_scaled[e % 2][:, :], w1[:, e, :],
                                        rms_cols[:, e:e + 1].to_broadcast([P, HIDDEN]),
                                        ALU.mult).then_inc(S["w1_scaled_ready"], 1)

            pool.wait_ge(S["rms_ready"], 1)
            pool.wait_ge(S["w1_loaded"], 32)
            for e in range(2):
                scale_w1(e)
            pool.wait_ge(S["pow_base_ready"], 1)
            pool.wait_ge(S["moe_consts_ready"], 1)
            nc.gpsimd.tensor_tensor(pow_out[:, :, :], pow_base[:, :, :], pow_exp[:, :, :], ALU.pow)\
                .then_inc(S["pow_ready"], 1)
            pool.wait_ge(S["hidden_filled"], 1)
            scale_w1(2)
            with pool.Fori(0, LOOP_STEPS) as i:
                for u in range(4):
                    e = i * 4 + (LOOP_FROM + u)
                    pool.wait_ge(S["hidden_filled"], e - 1)
                    nc.gpsimd.tensor_tensor(
                        w1_scaled[(LOOP_FROM + u) % 2][:, :],
                        w1[:, bass.ds(e, 1), :].rearrange("p a f -> p (a f)"),
                        rms_cols[:, bass.ds(e, 1)].to_broadcast([P, HIDDEN]), ALU.mult)\
                        .then_inc(S["w1_scaled_ready"], 1)
            pool.wait_ge(S["hidden_filled"], EXPERTS - 2)
            scale_w1(EXPERTS - 1)

        @block.tensor
        def _(pe):
            pe.wait_ge(S["ident_ready"], 1)

            def transpose_weights(name, src, n):
                job = f"{name}{n}"
                wait_bank_free(pe, job)
                for i in range(4):
                    c = 4 * n + i
                    last = nc.tensor.transpose(ring[:, bank_of(job), i * P:(i + 1) * P],
                                               src[:, c * P:(c + 1) * P], ident[:, :])
                last.then_inc(S["ring_filled"], 1)

            pe.wait_ge(S["wk_loaded"], 16)
            for n in range(2):
                transpose_weights("wkT", wk, n)
            pe.wait_ge(S["wq_loaded"], 16)
            for n in range(2):
                transpose_weights("wqT", wq, n)

            pe.wait_ge(S["ctx_head_loaded"], 16)
            wait_bank_free(pe, "ctxT")
            for b in range(B):
                last = nc.tensor.transpose(ring[:, bank_of("ctxT"), b * Q:(b + 1) * Q],
                                           ctx_head[:, b, :], ident[0:Q, 0:Q])
            last.then_inc(S["ring_filled"], 1)

            for g in range(GROUPS):
                if g % 2 == 0:
                    pe.wait_ge(*evacuated(f"wkT{g // 2}"))
                    pe.wait_ge(*evacuated(f"wqT{g // 2}"))
                wait_bank_free(pe, f"A{g}")
                r = HEAD * (g % 2)
                for i in range(4):
                    c = head_of(g, i) // 2
                    last = nc.tensor.matmul(ring[:, bank_of(f"A{g}"), i * D:(i + 1) * D],
                                            wkT[r:r + HEAD, c, :], wqT[r:r + HEAD, c, :],
                                            start=True, stop=True)
                last.then_inc(S["ring_filled"], 1)

            def project_keys(s):
                job = f"K{s}"
                if s % 4 == 0:
                    pe.wait_ge(*evacuated(f"A{s // 4}"))
                if s == 0:
                    pe.wait_ge(*evacuated("ctxT"))
                wait_bank_free(pe, job)
                nc.tensor.matmul(ring[:, bank_of(job), 0:B * Q], A_T[:, s, :], ctx_headT[:, :],
                                 start=True, stop=True).then_inc(S["ring_filled"], 1)

            for s in range(4):
                project_keys(s)
            pe.wait_ge(S["xn_ready"], 1)
            wait_bank_free(pe, "xnT")
            for t in range(PAIRS):
                last = nc.tensor.transpose(ring[:, bank_of("xnT"), t * ROWS:(t + 1) * ROWS],
                                           xn_rows[:, t, :], ident[0:ROWS, 0:ROWS])
            last.then_inc(S["ring_filled"], 1)
            for s in range(4, HEADS):
                project_keys(s)

            def scores(t):
                if t == 0:
                    pe.wait_ge(*evacuated("xnT"))
                else:
                    pe.wait_ge(S["scores_read"], 2 * t)
                for half in range(2):
                    if t == 0:
                        pe.wait_ge(*evacuated(f"K{8 * half + 7}"))
                        pe.wait_ge(*evacuated(f"K{8 * half + 6}"))
                    for bb in range(2):
                        b = 2 * t + bb
                        last = nc.tensor.matmul(
                            score_ps[bb * SLOT:(bb + 1) * SLOT, half, 0:8 * Q],
                            xnT[:, b, :], keyproj[:, 8 * half:8 * half + 8, b * Q:(b + 1) * Q],
                            start=True, stop=True)
                    last.then_inc(S["scores_ready"], 1)

            def transpose_probs(t):
                pe.wait_ge(S["probs_ready"], t + 1)
                for g in range(GROUPS):
                    job = f"P{t}.{g}"
                    wait_bank_free(pe, job)
                    for i in range(4):
                        last = nc.tensor.transpose(ring[0:Q, bank_of(job), i * P:(i + 1) * P],
                                                   probs[:, t % 2, 4 * g + i, :], ident[:, :])
                    last.then_inc(S["ring_filled"], 1)

            def mix_context(t):
                for half in range(2):
                    pe.wait_ge(*evacuated(f"P{t}.{2 * half}"))
                    pe.wait_ge(*evacuated(f"P{t}.{2 * half + 1}"))
                    for bb in range(2):
                        job = f"C{t}.{bb}.{half}"
                        wait_bank_free(pe, job)
                        nc.tensor.matmul(ring[:, bank_of(job), 0:8 * Q], ctx_head[:, 2 * t + bb, :],
                                         probsT[:, 8 * half:8 * half + 8, bb * Q:(bb + 1) * Q],
                                         start=True, stop=True).then_inc(S["ring_filled"], 1)

            def attention_out(t):
                if t == 0:
                    pe.wait_ge(*evacuated("M3"))
                    pe.wait_ge(*evacuated("M2"))
                else:
                    pe.wait_ge(S["x1_ready"], t)
                for s in range(HEADS):
                    if s % 8 == 0:
                        for bb in range(2):
                            pe.wait_ge(*evacuated(f"C{t}.{bb}.{s // 8}"))
                    last = nc.tensor.matmul(attn_ps[0:ROWS, 0:D], mixT[:, s, :], M[:, s, :],
                                            start=(s == 0), stop=(s == HEADS - 1))
                last.then_inc(S["attn_done"], 1)

            scores(0)
            pe.wait_ge(S["wv_loaded"], 16)
            for n in range(2):
                transpose_weights("wvT", wv, n)
            pe.wait_ge(S["wo_loaded"], 16)
            for g in range(GROUPS):
                if g % 2 == 0:
                    pe.wait_ge(*evacuated(f"wvT{g // 2}"))
                wait_bank_free(pe, f"M{g}")
                r = HEAD * (g % 2)
                for i in range(4):
                    c = head_of(g, i) // 2
                    last = nc.tensor.matmul(ring[:, bank_of(f"M{g}"), i * D:(i + 1) * D],
                                            wvT[r:r + HEAD, c, :], wo[r:r + HEAD, c, :],
                                            start=True, stop=True)
                last.then_inc(S["ring_filled"], 1)
            pe.wait_ge(S["rms_loaded"], 32)
            nc.tensor.transpose(misc_ps[:, 0:EXPERTS], rms_rows[:, :], ident[0:EXPERTS, 0:EXPERTS])\
                .then_inc(S["rms_filled"], 1)

            for t in range(PAIRS):
                if t + 1 < PAIRS:
                    scores(t + 1)
                transpose_probs(t)
                mix_context(t)
                if t == PAIRS - 1:
                    pe.wait_ge(S["guard_max_ready"], 1)
                    pe.wait_ge(S["rms_ready"], 1)
                    for k in range(2):
                        last = nc.tensor.transpose(misc_ps[0:1, k * P:(k + 1) * P],
                                                   guard_max[:, k:k + 1], ident[:, :])
                    last.then_inc(S["guard_rows_ready"], 1)
                attention_out(t)

            pe.wait_ge(S["guard_ready"], 1)
            ok = pe.value_load(guard_ok[0:1, 0:1], min_val=0, max_val=1)
            with pe.If(ok < 1):
                with pe.Fori(0, B) as b:
                    pe.wait_ge(S["g_batch_ready"], b + 1)
                    for c in range(KC):
                        last = nc.tensor.transpose(ring[:, c // 4, (c % 4) * KP:(c % 4 + 1) * KP],
                                                   g_ctx[:, c, :], ident[0:KP, 0:KP])
                    last.then_inc(S["g_ctxT_filled"], 1)
                    with pe.Fori(0, HEADS) as h:
                        n = b * HEADS + h
                        pe.wait_ge(S["g_ctxT_ready"], b + 1)
                        pe.wait_ge(S["g_A_ready"], n + 1)
                        for k in range(3):
                            last = nc.tensor.matmul(ring[:, k, 0:4 * KP], g_AT[:, :],
                                                    g_ctxT[:, k * 4 * KP:(k + 1) * 4 * KP],
                                                    start=True, stop=True)
                        last.then_inc(S["g_key_filled"], 1)
                        pe.wait_ge(S["g_key_ready"], n + 1)
                        for k in range(3):
                            last = nc.tensor.matmul(ring[0:Q, k, 0:4 * KP], g_xnT[:, :],
                                                    g_key[:, k * 4 * KP:(k + 1) * 4 * KP],
                                                    start=True, stop=True)
                        last.then_inc(S["g_score_filled"], 1)
                        pe.wait_ge(S["g_prob_ready"], n + 1)
                        for c in range(KC):
                            last = nc.tensor.matmul(
                                score_ps[0:KP, c // 8, (c % 8) * Q:(c % 8 + 1) * Q],
                                g_prob[:, c * KP:(c + 1) * KP], ident[0:Q, 0:Q],
                                start=True, stop=True)
                        last.then_inc(S["g_probT_filled"], 1)
                        pe.wait_ge(S["g_probT_ready"], n + 1)
                        for c in range(KC):
                            last = nc.tensor.matmul(attn_ps[:, 0:Q], g_ctx[:, c, :], g_probT[:, c, :],
                                                    start=(c == 0), stop=(c == KC - 1))
                        last.then_inc(S["g_mix_filled"], 1)
                        pe.wait_ge(S["g_mix_ready"], n + 1)
                        nc.tensor.matmul(misc_ps[0:Q, 0:D], g_mixT[:, :],
                                         M[:, bass.ds(h, 1), :].rearrange("p a d -> p (a d)"),
                                         start=True, stop=True).then_inc(S["g_out_filled"], 1)
                pe.wait_ge(S["g_vector_steps"], B * G_BATCH_STEPS)

            pe.wait_ge(S["h_ready"], 1)
            for t in range(PAIRS):
                last = nc.tensor.transpose(attn_ps[:, t * ROWS:(t + 1) * ROWS], h_rows[:, t, :],
                                           ident[0:ROWS, 0:ROWS])
            last.then_inc(S["hT_filled"], 1)
            pe.wait_ge(S["hT_ready"], 1)
            pe.wait_ge(S["router_loaded"], 16)
            for t in range(PAIRS):
                last = nc.tensor.matmul(misc_ps[0:ROWS, t * ROUTED:(t + 1) * ROUTED],
                                        hT[:, t * ROWS:(t + 1) * ROWS], router_w[:, :],
                                        start=True, stop=True)
            last.then_inc(S["logits_filled"], 1)

            def hidden_products(slot):
                for c in range(2):
                    last = nc.tensor.matmul(ring[:, 2 * slot + c, 0:TOKENS],
                                            w1_scaled[slot][:, c * P:(c + 1) * P], hT[:, :],
                                            start=True, stop=True)
                last.then_inc(S["hidden_filled"], 1)

            def expert_output(slot, w2_chunk):
                for t in range(PAIRS):
                    for c in range(2):
                        last = nc.tensor.matmul(score_ps[0:ROWS, slot, t * D:(t + 1) * D],
                                                hidden[slot][:, c, t * ROWS:(t + 1) * ROWS],
                                                w2_chunk(c), start=(c == 0), stop=(c == 1))
                last.then_inc(S["expert_done"], 1)

            def static_w2(e):
                return lambda c: w2[:, e, c, :]

            pe.wait_ge(S["w1_scaled_ready"], 1)
            hidden_products(0)
            pe.wait_ge(S["w1_scaled_ready"], 2)
            hidden_products(1)
            pe.wait_ge(S["w2_loaded"], 32)
            pe.wait_ge(S["hidden_ready"], 1)
            expert_output(0, static_w2(0))
            pe.wait_ge(S["w1_scaled_ready"], 3)
            hidden_products(0)
            pe.wait_ge(S["hidden_ready"], 2)
            expert_output(1, static_w2(1))
            with pe.Fori(0, LOOP_STEPS) as i:
                for u in range(4):
                    e = i * 4 + (LOOP_FROM + u)
                    slot = (LOOP_FROM + u) % 2
                    pe.wait_ge(S["w1_scaled_ready"], e + 1)
                    pe.wait_ge(S["hidden_ready"], e - 1)
                    hidden_products(slot)
                    pe.wait_ge(S["hidden_ready"], e)
                    pe.wait_ge(S["acc_done"], e - 2)
                    expert_output(1 - slot, lambda c: w2[:, bass.ds(e - 1, 1), c, :]
                                  .rearrange("p a n -> p (a n)"))
            pe.wait_ge(S["w1_scaled_ready"], EXPERTS)
            pe.wait_ge(S["hidden_ready"], EXPERTS - 2)
            hidden_products((EXPERTS - 1) % 2)
            for e in range(EXPERTS - 2, EXPERTS):
                pe.wait_ge(S["hidden_ready"], e + 1)
                pe.wait_ge(S["acc_done"], e - 1)
                expert_output(e % 2, static_w2(e))

        @block.scalar
        def _(act):
            act.dma_start(x_rows[:, :, :],
                          A["x"].rearrange("b q d -> (b q) d").rearrange("(t p) d -> p t d", p=ROWS))\
                .then_inc(S["x_loaded"], 16)
            act.dma_start(ctx_head[:, :, :],
                          A["ctx_1024"][:, 0:Q, :].rearrange("b k d -> k b d"))\
                .then_inc(S["ctx_head_loaded"], 16)
            act.dma_start(gate_col[:, 0:1], A["g_xattn"].partition_broadcast(P))\
                .then_inc(S["gates_loaded"], 16)
            act.dma_start(gate_col[:, 1:2], A["g_ffn"].partition_broadcast(P))\
                .then_inc(S["gates_loaded"], 16)
            act.dma_start(rms_rows[0:SHARED, :], A["L0_ffn_rms_w_s"]).then_inc(S["rms_loaded"], 16)
            act.dma_start(rms_rows[SHARED:EXPERTS, :], A["L0_ffn_rms_w"])\
                .then_inc(S["rms_loaded"], 16)
            act.dma_start(router_w[:, :], A["L0_ffn_router_w"]).then_inc(S["router_loaded"], 16)

            def evacuate_own(jobs):
                for job in jobs:
                    if job in ACT_JOBS:
                        dst, src = evacuation(job)
                        wait_filled(act, job)
                        nc.scalar.activation(dst, src, ACT.Copy).then_inc(S["act_drained"], 1)

            def square_sum(n, column, src):
                if n:
                    act.wait_ge(S["squares_done"], n)
                rows, cols = src.shape[0], src.shape[1]
                nc.scalar.activation(square_junk[0:rows, 0:cols], src, ACT.Square,
                                     accum_out=guard_parts[0:rows, column:column + 1])\
                    .then_inc(S["squares_done"], 1)

            def context_squares(batches):
                for b in batches:
                    act.wait_ge(ctx_loaded[b], 16)
                    square_sum(GROUPS + b, GROUPS + b, ctx_all[:, b, :])

            def softmax_exp(t):
                act.wait_ge(S["shifted_ready"], t + 1)
                nc.scalar.activation(probs[:, t % 2, :, :], probs[:, t % 2, :, :], ACT.Exp)\
                    .then_inc(S["exp_ready"], 1)

            cut = [RING_JOBS.index(j) for j in ("K8", "wvT0", "P0.0")]
            evacuate_own(RING_JOBS[:cut[0]])
            act.wait_ge(S["gates_loaded"], 32)
            nc.scalar.activation(tanh_col[:, :], gate_col[:, :], ACT.Tanh).then_inc(S["tanh_ready"], 1)
            act.wait_ge(S["causal_zero"], 1)
            for g in range(GROUPS):
                act.wait_ge(*evacuated(f"A{g}"))
                square_sum(g, g, A_T[:, 4 * g:4 * g + 4, :].rearrange("p h d -> p (h d)"))
            evacuate_own(RING_JOBS[cut[0]:cut[1]])
            evacuate_own(RING_JOBS[cut[1]:cut[2]])
            softmax_exp(0)
            for t in range(PAIRS):
                evacuate_own([f"P{t}.{g}" for g in range(GROUPS)])
                if t + 1 < PAIRS:
                    softmax_exp(t + 1)
                evacuate_own([f"C{t}.{bb}.{half}" for half in range(2) for bb in range(2)])
                context_squares([range(0, 3), range(3, 6), range(6, 8), []][t])

            act.wait_ge(S["guard_ready"], 1)
            ok = act.value_load(guard_ok[0:1, 0:1], min_val=0, max_val=1)
            with act.If(ok < 1):
                with act.Fori(0, B) as b:
                    act.wait_ge(S["g_ctxT_filled"], b + 1)
                    nc.scalar.activation(g_ctxT.rearrange("p (k n) -> p k n", k=3),
                                         ring[:, 0:3, 0:4 * KP], ACT.Copy)\
                        .then_inc(S["g_ctxT_ready"], 1)
                    with act.Fori(0, HEADS) as h:
                        n = b * HEADS + h
                        act.wait_ge(S["g_key_filled"], n + 1)
                        nc.scalar.activation(g_key.rearrange("p (k n) -> p k n", k=3),
                                             ring[:, 0:3, 0:4 * KP], ACT.Copy)\
                            .then_inc(S["g_key_ready"], 1)
                        act.wait_ge(S["g_max_ready"], n + 1)
                        nc.scalar.activation(g_prob, g_prob, ACT.Exp, bias=g_max[:, 0:1],
                                             accum_out=g_sum[:, 0:1]).then_inc(S["g_exp_ready"], 1)
                        act.wait_ge(S["g_probT_filled"], n + 1)
                        nc.scalar.activation(g_probT[:, 0:8, :].rearrange("p c q -> p (c q)"),
                                             score_ps[0:KP, 0, 0:8 * Q], ACT.Copy)
                        nc.scalar.activation(g_probT[:, 8:KC, :].rearrange("p c q -> p (c q)"),
                                             score_ps[0:KP, 1, 0:(KC - 8) * Q], ACT.Copy)\
                            .then_inc(S["g_probT_ready"], 1)
                        act.wait_ge(S["g_mix_filled"], n + 1)
                        nc.scalar.activation(g_mixT[:, :], attn_ps[:, 0:Q], ACT.Copy)\
                            .then_inc(S["g_mix_ready"], 1)
                    act.wait_ge(S["g_vector_steps"], (b + 1) * G_BATCH_STEPS)
                    act.dma_start(g_attn_dram[bass.ds(b * Q, Q), :], g_acc[:, :])\
                        .then_inc(S["g_stored"], 16)
                act.wait_ge(S["g_stored"], 16 * B)
                act.dma_start(attn_all[:, :, :], g_attn_dram.rearrange("(t p) d -> p t d", p=ROWS))\
                    .then_inc(S["g_loaded"], 16)
                act.wait_ge(S["g_loaded"], 16)

            act.wait_ge(S["hT_filled"], 1)
            nc.scalar.activation(hT[:, :], attn_ps[:, 0:TOKENS], ACT.Copy).then_inc(S["hT_ready"], 1)
            act.wait_ge(S["logits_ready"], 1)
            nc.scalar.activation(expo[:, :, :], shifted[:, :, :], ACT.Exp)\
                .then_inc(S["router_exp_ready"], 1)

            def silu(slot):
                nc.scalar.activation(hidden[slot], ring[:, 2 * slot:2 * slot + 2, 0:TOKENS],
                                     ACT.Silu).then_inc(S["hidden_ready"], 1)

            for e in range(LOOP_FROM):
                act.wait_ge(S["hidden_filled"], e + 1)
                if e >= 2:
                    act.wait_ge(S["expert_done"], e - 1)
                silu(e % 2)
            with act.Fori(0, LOOP_STEPS) as i:
                for u in range(4):
                    e = i * 4 + (LOOP_FROM + u)
                    act.wait_ge(S["hidden_filled"], e + 1)
                    act.wait_ge(S["expert_done"], e - 1)
                    silu((LOOP_FROM + u) % 2)
            act.wait_ge(S["hidden_filled"], EXPERTS)
            act.wait_ge(S["expert_done"], EXPERTS - 2)
            silu((EXPERTS - 1) % 2)

        @block.vector
        def _(dve):
            steps = [0]

            def then_wait(instruction):
                steps[0] += 1
                instruction.then_inc(S["vector_steps"], 1)
                dve.wait_ge(S["vector_steps"], steps[0])

            def evacuate_own(jobs):
                for job in jobs:
                    if job in DVE_JOBS:
                        dst, src = evacuation(job)
                        wait_filled(dve, job)
                        nc.vector.tensor_copy(dst, src).then_inc(S["dve_drained"], 1)

            def moments(rows):
                for t in range(PAIRS):
                    last = nc.vector.bn_stats(ln_stats[:, t, :], rows[:, t, :])
                then_wait(last)
                for t in range(PAIRS):
                    last = nc.vector.bn_aggr(ln_mv[:, t, :], ln_stats[:, t, :])
                then_wait(last)

            dve.wait_ge(S["x_loaded"], 16)
            moments(x_rows)
            nc.vector.tensor_scalar(ln_var[:, :], ln_mv[:, :, 1], LN_EPS, None, ALU.add)\
                .then_inc(S["ln1_var_ready"], 1)
            cut = [RING_JOBS.index(j) for j in ("K0", "wvT0", "P0.0")]
            evacuate_own(RING_JOBS[:cut[0]])
            dve.wait_ge(S["ln1_rstd_ready"], 1)
            for t in range(PAIRS):
                last = nc.vector.tensor_scalar(xn_rows[:, t, :], x_rows[:, t, :], ln_mv[:, t, 0:1],
                                               ln_rstd[:, t:t + 1], ALU.subtract, ALU.mult)
            last.then_inc(S["xn_ready"], 1)
            dve.wait_ge(S["slots_zero"], 1)
            evacuate_own(RING_JOBS[cut[0]:cut[1]])
            dve.wait_ge(S["causal_ready"], 1)

            def softmax_shift(t):
                p = probs[:, t % 2, :, :]
                if t >= 2:
                    dve.wait_ge(S["ring_filled"], RING_JOBS.index(f"P{t - 2}.{GROUPS - 1}") + 1)
                for half in range(2):
                    dve.wait_ge(S["scores_ready"], 2 * t + half + 1)
                    nc.vector.scalar_tensor_tensor(
                        out=probs[:, t % 2, 8 * half:8 * half + 8, :],
                        in0=score_ps[:, half, 0:8 * Q].rearrange("p (h k) -> p h k", h=8),
                        scalar=SCALE, in1=causal[:, :].unsqueeze(1).to_broadcast([P, 8, Q]),
                        op0=ALU.mult, op1=ALU.add).then_inc(S["scores_read"], 1)
                dve.wait_ge(S["scores_read"], 2 * t + 2)
                then_wait(nc.vector.tensor_reduce(row_max[:, :], p, AX.X, ALU.max))
                nc.vector.tensor_tensor(p, p, row_max[:, :].unsqueeze(2).to_broadcast([P, HEADS, Q]),
                                        ALU.subtract).then_inc(S["shifted_ready"], 1)

            def softmax_normalise(t):
                p = probs[:, t % 2, :, :]
                dve.wait_ge(S["exp_ready"], t + 1)
                then_wait(nc.vector.tensor_reduce(row_sum[:, :], p, AX.X, ALU.add))
                then_wait(nc.vector.reciprocal(row_inv[:, :], row_sum[:, :]))
                nc.vector.tensor_tensor(p, p, row_inv[:, :].unsqueeze(2).to_broadcast([P, HEADS, Q]),
                                        ALU.mult).then_inc(S["probs_ready"], 1)

            def first_residual(t):
                dve.wait_ge(S["attn_done"], t + 1)
                nc.vector.scalar_tensor_tensor(out=x1[:, t, :], in0=attn_ps[0:ROWS, 0:D],
                                               scalar=tanh_col[0:ROWS, 0:1], in1=x_rows[:, t, :],
                                               op0=ALU.mult, op1=ALU.add)\
                    .then_inc(S["x1_ready"], 1)

            softmax_shift(0)
            evacuate_own(RING_JOBS[cut[1]:cut[2]])
            softmax_normalise(0)
            dve.wait_ge(S["rms_filled"], 1)
            nc.vector.tensor_copy(rms_cols[:, :], misc_ps[:, 0:EXPERTS]).then_inc(S["rms_ready"], 1)
            dve.wait_ge(S["tanh_ready"], 1)
            for t in range(PAIRS):
                if t + 1 < PAIRS:
                    softmax_shift(t + 1)
                    softmax_normalise(t + 1)
                else:
                    dve.wait_ge(S["squares_done"], GROUPS + B)
                    nc.vector.tensor_reduce(guard_max[:, 0:1], guard_parts[:, 0:GROUPS], AX.X, ALU.max)
                    nc.vector.tensor_reduce(guard_max[:, 1:2], guard_parts[:, GROUPS:GROUPS + B],
                                            AX.X, ALU.max).then_inc(S["guard_max_ready"], 1)
                    dve.wait_ge(S["guard_rows_ready"], 1)
                    then_wait(nc.vector.tensor_reduce(
                        guard_pair[:, :], misc_ps[0:1, 0:2 * P].rearrange("p (k n) -> p k n", k=2),
                        AX.X, ALU.max))
                    then_wait(nc.vector.tensor_tensor(guard_prod[:, :], guard_pair[:, 0:1],
                                                      guard_pair[:, 1:2], ALU.mult))
                    nc.vector.tensor_scalar(guard_ok[:, :], guard_prod[:, :], GUARD_LIMIT, None,
                                            ALU.is_lt).then_inc(S["guard_ready"], 1)
                first_residual(t)

            dve.wait_ge(S["guard_ready"], 1)
            ok = dve.value_load(guard_ok[0:1, 0:1], min_val=0, max_val=1)
            with dve.If(ok < 1):
                with dve.Fori(0, B) as b:
                    nc.vector.memset(g_acc[:, :], 0.0).then_inc(S["g_vector_steps"], 1)
                    nc.vector.tensor_copy(g_xnT[:, :], xnT[:, bass.ds(b, 1), 0:Q]
                                          .rearrange("p a q -> p (a q)"))
                    nc.vector.tensor_copy(g_ctx.rearrange("p c d -> p (c d)"),
                                          ctx_all[:, bass.ds(b, 1), :].rearrange("p a n -> p (a n)"))\
                        .then_inc(S["g_batch_ready"], 1)
                    with dve.Fori(0, HEADS) as h:
                        n = b * HEADS + h
                        done = b * G_BATCH_STEPS + h * G_HEAD_STEPS + 1
                        nc.vector.tensor_copy(g_AT[:, :], A_T[:, bass.ds(h, 1), :]
                                              .rearrange("p a d -> p (a d)"))\
                            .then_inc(S["g_A_ready"], 1)
                        dve.wait_ge(S["g_score_filled"], n + 1)
                        nc.vector.tensor_scalar(g_prob.rearrange("p (k n) -> p k n", k=3),
                                                ring[0:Q, 0:3, 0:4 * KP], SCALE, MASKED,
                                                ALU.mult, ALU.add).then_inc(S["g_vector_steps"], 1)
                        dve.wait_ge(S["g_vector_steps"], done + 1)
                        for k in range(3):
                            src = ring[0:Q, k, 0:4 * KP].rearrange("p (c n) -> p c n", c=4)
                            dst = g_prob[:, k * 4 * KP:(k + 1) * 4 * KP]
                            last = nc.vector.scalar_tensor_tensor(
                                out=dst.rearrange("p (c n) -> p c n", c=4)[:, :, 0:5],
                                in0=src[:, :, 0:5], scalar=SCALE,
                                in1=causal_all[:, 4 * k:4 * k + 4, :], op0=ALU.mult, op1=ALU.add)
                        last.then_inc(S["g_vector_steps"], 1)
                        dve.wait_ge(S["g_vector_steps"], done + 2)
                        nc.vector.tensor_reduce(g_max[:, :], g_prob, AX.X, ALU.max, negate=True)\
                            .then_inc(S["g_max_ready"], 1)
                        dve.wait_ge(S["g_exp_ready"], n + 1)
                        nc.vector.reciprocal(g_inv[:, :], g_sum[:, :])\
                            .then_inc(S["g_vector_steps"], 1)
                        dve.wait_ge(S["g_vector_steps"], done + 3)
                        nc.vector.tensor_scalar(g_prob, g_prob, g_inv[:, 0:1], None, ALU.mult)\
                            .then_inc(S["g_prob_ready"], 1)
                        dve.wait_ge(S["g_out_filled"], n + 1)
                        nc.vector.tensor_tensor(g_acc[:, :], g_acc[:, :], misc_ps[0:Q, 0:D], ALU.add)\
                            .then_inc(S["g_vector_steps"], 1)
                    dve.wait_ge(S["g_stored"], (b + 1) * 16)
                dve.wait_ge(S["g_loaded"], 16)
                for t in range(PAIRS):
                    last = nc.vector.scalar_tensor_tensor(
                        out=x1[:, t, :], in0=attn_all[:, t, :], scalar=tanh_col[0:ROWS, 0:1],
                        in1=x_rows[:, t, :], op0=ALU.mult, op1=ALU.add)
                last.then_inc(S["g_x1_ready"], 1)
                dve.wait_ge(S["g_x1_ready"], 1)

            dve.wait_ge(S["x1_ready"], PAIRS)
            moments(x1)
            nc.vector.tensor_scalar(pow_base[:, 0:2, :],
                                    ln_mv[:, :, 1].unsqueeze(1).to_broadcast([ROWS, 2, PAIRS]),
                                    1.0 + RMS_EPS, LN_EPS * RMS_EPS, ALU.mult, ALU.add)
            nc.vector.tensor_scalar(pow_base[:, 2, :], ln_mv[:, :, 1], LN_EPS, None, ALU.add)\
                .then_inc(S["pow_base_ready"], 1)
            dve.wait_ge(S["pow_ready"], 1)
            for t in range(PAIRS):
                last = nc.vector.tensor_scalar(h_rows[:, t, :], x1[:, t, :], ln_mv[:, t, 0:1],
                                               pow_out[:, 0, t:t + 1], ALU.subtract, ALU.mult)
            last.then_inc(S["h_ready"], 1)
            then_wait(nc.vector.tensor_tensor(ratio[:, :], pow_out[:, 1, :], pow_out[:, 2, :],
                                              ALU.mult))

            def wide(col):
                return col[:, :].unsqueeze(2).to_broadcast([ROWS, PAIRS, ROUTED])

            dve.wait_ge(S["logits_filled"], 1)
            then_wait(nc.vector.tensor_tensor(
                logits[:, :, :],
                misc_ps[0:ROWS, 0:PAIRS * ROUTED].rearrange("p (t e) -> p t e", t=PAIRS),
                wide(ratio), ALU.mult))
            then_wait(nc.vector.tensor_reduce(logit_max[:, :], logits[:, :, :], AX.X, ALU.max))
            nc.vector.tensor_tensor(shifted[:, :, :], logits[:, :, :], wide(logit_max), ALU.subtract)\
                .then_inc(S["logits_ready"], 1)
            dve.wait_ge(S["router_exp_ready"], 1)
            dve.wait_ge(S["moe_consts_ready"], 1)
            nc.vector.tensor_reduce(exp_sum[:, :], expo[:, :, :], AX.X, ALU.add)
            for i, values in enumerate((expo, rest)):
                then_wait(nc.vector.tensor_reduce(top[i][:, :], values[:, :, :], AX.X, ALU.max))
                then_wait(nc.vector.tensor_tensor(hit[i][:, :, :], values[:, :, :], wide(top[i]),
                                                  ALU.is_ge))
                then_wait(nc.vector.tensor_tensor(tie[i][:, :, :], hit[i][:, :, :], rank[:, :, :],
                                                  ALU.mult))
                then_wait(nc.vector.tensor_reduce(best_rank[i][:, :], tie[i][:, :, :], AX.X, ALU.max))
                then_wait(nc.vector.tensor_tensor(pick[i][:, :, :], tie[i][:, :, :],
                                                  wide(best_rank[i]), ALU.is_equal))
                if i == 0:
                    then_wait(nc.vector.scalar_tensor_tensor(
                        out=rest[:, :, :], in0=pick[0][:, :, :], scalar=-2.0, in1=expo[:, :, :],
                        op0=ALU.mult, op1=ALU.add))
            then_wait(nc.vector.tensor_tensor(pick[0][:, :, :], pick[0][:, :, :], pick[1][:, :, :],
                                              ALU.add))
            then_wait(nc.vector.tensor_tensor(chosen[:, :, :], pick[0][:, :, :], expo[:, :, :],
                                              ALU.mult))
            then_wait(nc.vector.tensor_reduce(top_sum[:, :], chosen[:, :, :], AX.X, ALU.add))
            then_wait(nc.vector.scalar_tensor_tensor(out=gate_den[:, :], in0=exp_sum[:, :],
                                                     scalar=GATE_EPS, in1=top_sum[:, :],
                                                     op0=ALU.mult, op1=ALU.add))
            then_wait(nc.vector.reciprocal(gate_inv[:, :], gate_den[:, :]))
            then_wait(nc.vector.tensor_tensor(
                gates[:, SHARED:EXPERTS, :].rearrange("p e t -> p t e"), chosen[:, :, :],
                wide(gate_inv), ALU.mult))

            def add_expert(slot, gate):
                for t in range(PAIRS):
                    last = nc.vector.scalar_tensor_tensor(
                        out=moe[:, t, :], in0=score_ps[0:ROWS, slot, t * D:(t + 1) * D],
                        scalar=gate(t), in1=moe[:, t, :], op0=ALU.mult, op1=ALU.add)
                last.then_inc(S["acc_done"], 1)

            def static_gate(e):
                return lambda t: gates[:, e, t:t + 1]

            dve.wait_ge(S["expert_done"], 1)
            nc.vector.tensor_copy(moe[:, :, :].rearrange("p t d -> p (t d)"), score_ps[0:ROWS, 0, :])\
                .then_inc(S["acc_done"], 1)
            for e in range(1, LOOP_FROM):
                dve.wait_ge(S["expert_done"], e + 1)
                dve.wait_ge(S["acc_done"], e)
                add_expert(e % 2, static_gate(e))
            with dve.Fori(0, LOOP_STEPS) as i:
                for u in range(4):
                    e = i * 4 + (LOOP_FROM + u)
                    dve.wait_ge(S["expert_done"], e + 1)
                    dve.wait_ge(S["acc_done"], e)
                    add_expert((LOOP_FROM + u) % 2, lambda t: gates[:, bass.ds(e, 1), t]
                               .rearrange("p a -> p a"))
            dve.wait_ge(S["expert_done"], EXPERTS)
            dve.wait_ge(S["acc_done"], EXPERTS - 1)
            add_expert((EXPERTS - 1) % 2, static_gate(EXPERTS - 1))
            dve.wait_ge(S["acc_done"], EXPERTS)
            for t in range(PAIRS):
                nc.vector.scalar_tensor_tensor(out=result[:, t, :], in0=moe[:, t, :],
                                               scalar=tanh_col[0:ROWS, 1:2], in1=x1[:, t, :],
                                               op0=ALU.mult, op1=ALU.add)\
                    .then_inc(S["result_ready"], 1)


_INS = ["x", "ctx_1024", "g_xattn", "g_ffn", "L0_xattn_w_q", "L0_xattn_w_k", "L0_xattn_w_v",
        "L0_xattn_w_o", "L0_ffn_router_w", "L0_ffn_rms_w", "L0_ffn_w1", "L0_ffn_w2",
        "L0_ffn_rms_w_s", "L0_ffn_w1_s", "L0_ffn_w2_s"]


def kernel(**inputs):
    import numpy as _np
    import concourse.bacc as _bacc
    from concourse import mybir as _mybir
    from concourse.bass_utils import run_bass_kernel_spmd as _run

    nc = _bacc.Bacc("TRN2", target_bir_lowering=False, num_devices=1)
    arrays, args = {}, {}
    for name in _INS:
        a = _np.ascontiguousarray(inputs[name])
        arrays[f"in_{name}_dram"] = a
        args[name] = nc.dram_tensor(f"in_{name}_dram", a.shape, _mybir.dt.from_np(a.dtype),
                                    kind="ExternalInput").ap()
    out = nc.dram_tensor("out_0_dram", (B, Q, D), _mybir.dt.float32, kind="ExternalOutput").ap()
    build(nc, args, out)
    r = _run(nc, [arrays], core_ids=[0])
    return r.results[0]["out_0_dram"]
```

```python
from contextlib import ExitStack

import concourse.bass as bass
from concourse import mybir

FP32 = mybir.dt.float32
FP32R = mybir.dt.float32r
INT32 = mybir.dt.int32
ACT = mybir.ActivationFunctionType
ALU = mybir.AluOpType
AX = mybir.AxisListType

B, Q, D = 8, 56, 128
KEYS = 1500
HEADS, HEAD = 16, 64
INNER = HEADS * HEAD
ROUTED, SHARED, HIDDEN = 14, 2, 256
EXPERTS = ROUTED + SHARED
TOKENS = B * Q
P = 128
PAIRS = B // 2
ROWS = 2 * Q
SLOT = 64
BANK = 512
KC = 12
KP = KEYS // KC
CHUNKS = INNER // P
GROUPS = HEADS // 4

SCALE = HEAD ** -0.5
MASKED = -10000.0
LN_EPS = 1e-5
RMS_EPS = 1.1920929e-07
GATE_EPS = 1e-9

SCORE_LIMIT = 4900.0
GUARD_LIMIT = SCORE_LIMIT ** 2 / (SCALE ** 2 * D * P)


def head_of(group, i):
    return 8 * (group // 2) + 2 * i + group % 2


RING_JOBS = (
    ["wkT0", "wkT1", "wqT0", "wqT1", "ctxT"]
    + [f"A{g}" for g in range(GROUPS)]
    + [f"K{s}" for s in range(4)] + ["xnT"] + [f"K{s}" for s in range(4, HEADS)]
    + ["wvT0", "wvT1"] + [f"M{g}" for g in range(GROUPS)]
)
for _t in range(PAIRS):
    RING_JOBS += [f"P{_t}.{g}" for g in range(GROUPS)]
    RING_JOBS += [f"C{_t}.{bb}.{half}" for half in range(2) for bb in range(2)]
RING_BANKS = 4
WARM_PRODUCTS = 8
GUARD_AT = PAIRS - 2
LOOP_FROM = 3
LOOP_STEPS = (EXPERTS - LOOP_FROM - 1) // 4
G_HEAD_STEPS = 4
G_BATCH_STEPS = 1 + HEADS * G_HEAD_STEPS
ACT_JOBS = [j for n, j in enumerate(RING_JOBS) if j[0] in "PC" or (n % 2 == 0 and j != "xnT")]
DVE_JOBS = [j for j in RING_JOBS if j not in ACT_JOBS]


def build(nc, A, out):
    ctx = ExitStack()
    with ctx:
        def sb(name, shape, dt=FP32):
            return ctx.enter_context(nc.sbuf_tensor(name, shape, dt))

        def pb(name, shape, dt=FP32):
            return ctx.enter_context(nc.psum_tensor(name, shape, dt))

        def sem(name):
            return ctx.enter_context(nc.semaphore(name))

        wq = sb("wq", [P, INNER])
        wk = sb("wk", [P, INNER])
        wv = wk
        wo = sb("wo", [P, CHUNKS, D])
        wqT = sb("wqT", [P, CHUNKS, D])
        wkT = sb("wkT", [P, CHUNKS, D])
        wvT = wkT
        A_T = sb("A_T", [P, HEADS, D])
        M = sb("M", [P, HEADS, D])
        x_rows = sb("x_rows", [ROWS, PAIRS, D])
        xn_rows = sb("xn_rows", [ROWS, PAIRS, D])
        xnT = sb("xnT", [P, B, SLOT])
        ctx_head = sb("ctx_head", [Q, B, D])
        ctx_headT = sb("ctx_headT", [P, B * Q])
        ctx_all = sb("ctx_all", [KP, B, KC * D])
        keyproj = sb("keyproj", [P, HEADS, B * Q])
        probs = sb("probs", [P, 2, HEADS, Q])
        probsT = sb("probsT", [Q, HEADS, ROWS])
        mixT = sb("mixT", [P, HEADS, ROWS])
        hidden_slots = sb("hidden_slots", [P, 2, 2, TOKENS])
        hidden = [hidden_slots[:, s, :, :] for s in range(2)]
        square_junk = hidden_slots[:, :, :, :].rearrange("p s c n -> p (s c n)")
        ident = sb("ident", [P, P])
        causal = sb("causal", [P, Q])
        causal_all = sb("causal_all", [Q, KC, 5])
        row_max = sb("row_max", [P, HEADS])
        row_sum = sb("row_sum", [P, HEADS])
        row_inv = sb("row_inv", [P, HEADS])
        ln_stats = sb("ln_stats", [ROWS, PAIRS, 6])
        ln_mv = sb("ln_mv", [ROWS, PAIRS, 2])
        ln_var = sb("ln_var", [ROWS, PAIRS])
        ln_rstd = sb("ln_rstd", [ROWS, PAIRS])
        minus_half = sb("minus_half", [ROWS, PAIRS])
        gate_col = sb("gate_col", [P, 2])
        tanh_col = sb("tanh_col", [P, 2])
        guard_parts = sb("guard_parts", [P, GROUPS + B])
        guard_max = sb("guard_max", [P, 2])
        guard_pair = sb("guard_pair", [1, 2])
        guard_prod = sb("guard_prod", [1, 1])
        guard_ok = sb("guard_ok", [1, 1], INT32)
        x1 = sb("x1", [ROWS, PAIRS, D])
        router_w = sb("router_w", [P, ROUTED])
        rms_rows = sb("rms_rows", [EXPERTS, D])
        rms_cols = sb("rms_cols", [P, EXPERTS])
        w1 = sb("w1", [P, EXPERTS, HIDDEN])
        w2 = sb("w2", [P, EXPERTS, 2, D])
        w1_full = sb("w1_full", [P, HIDDEN])
        w1_hi = [sb(f"w1_hi{s}", [P, HIDDEN], FP32R) for s in range(2)]
        w1_lo = [sb(f"w1_lo{s}", [P, HIDDEN], FP32R) for s in range(2)]
        h_base = sb("h_base", [ROWS, PAIRS])
        h_scale = sb("h_scale", [ROWS, PAIRS])
        ln2_var = sb("ln2_var", [ROWS, PAIRS])
        ln2_inv = sb("ln2_inv", [ROWS, PAIRS])
        ratio_square = sb("ratio_square", [ROWS, PAIRS])
        half = sb("half", [ROWS, PAIRS])
        warm = sb("warm", [P, P])
        ratio = sb("ratio", [ROWS, PAIRS])
        h_rows = sb("h_rows", [ROWS, PAIRS, D])
        hT = sb("hT", [P, TOKENS])
        hT_hi = sb("hT_hi", [P, TOKENS], FP32R)
        hT_lo = sb("hT_lo", [P, TOKENS], FP32R)
        logits = sb("logits", [ROWS, PAIRS, ROUTED])
        shifted = sb("shifted", [ROWS, PAIRS, ROUTED])
        expo = sb("expo", [ROWS, PAIRS, ROUTED])
        rank = sb("rank", [ROWS, PAIRS, ROUTED])
        hit = [sb(f"hit{i}", [ROWS, PAIRS, ROUTED]) for i in range(2)]
        tie = [sb(f"tie{i}", [ROWS, PAIRS, ROUTED]) for i in range(2)]
        pick = [sb(f"pick{i}", [ROWS, PAIRS, ROUTED]) for i in range(2)]
        rest = sb("rest", [ROWS, PAIRS, ROUTED])
        chosen = sb("chosen", [ROWS, PAIRS, ROUTED])
        top = [sb(f"top{i}", [ROWS, PAIRS]) for i in range(2)]
        best_rank = [sb(f"best_rank{i}", [ROWS, PAIRS]) for i in range(2)]
        logit_max = sb("logit_max", [ROWS, PAIRS])
        exp_sum = sb("exp_sum", [ROWS, PAIRS])
        top_sum = sb("top_sum", [ROWS, PAIRS])
        gate_den = sb("gate_den", [ROWS, PAIRS])
        gate_inv = sb("gate_inv", [ROWS, PAIRS])
        gates = sb("gates", [ROWS, EXPERTS, PAIRS])
        moe = sb("moe", [ROWS, PAIRS, D])

        def lay(space, at, rows, n):
            return space[0:rows, at:at + n]

        key_space = keyproj[:, :, :].rearrange("p h n -> p (h n)")
        prob_space = probs[:, :, :, :].rearrange("p s h k -> p (s h k)")
        mix_space = mixT[:, :, :].rearrange("p h n -> p (h n)")
        g_ctx = lay(key_space, 0, KP, KC * D).rearrange("p (c d) -> p c d", c=KC)
        g_ctxT = lay(key_space, 1536, P, KEYS)
        g_key = lay(key_space, 3072, P, KEYS)
        g_prob = lay(key_space, 4608, Q, KEYS)
        g_probT = lay(key_space, 6144, KP, KC * Q).rearrange("p (c q) -> p c q", c=KC)
        g_xnT = lay(prob_space, 0, P, Q)
        g_AT = lay(prob_space, 128, P, D)
        g_mixT = lay(prob_space, 256, P, Q)
        g_acc = lay(prob_space, 384, Q, D)
        attn_all = lay(mix_space, 0, ROWS, PAIRS * D).rearrange("p (t d) -> p t d", t=PAIRS)
        g_max = sb("g_max", [Q, 1])
        g_sum = sb("g_sum", [Q, 1])
        g_inv = sb("g_inv", [Q, 1])
        g_attn_dram = nc.dram_tensor("g_attn_dram", [TOKENS, D], FP32, kind="Internal").ap()

        ring = pb("ring", [P, RING_BANKS, BANK])
        score_ps = pb("score_ps", [P, 2, BANK])
        attn_ps = pb("attn_ps", [P, BANK])
        misc_ps = pb("misc_ps", [P, BANK])

        first_tiles = (PAIRS - 1) * ROWS
        h_parts = [(range(PAIRS - 1), slice(0, first_tiles), misc_ps),
                   ([PAIRS - 1], slice(first_tiles, TOKENS), attn_ps)]

        last_tiles = [bank_tile[0:ROWS, 0:D] for bank_tile in
                      (score_ps[:, (EXPERTS - 1) % 2, :], misc_ps[:, :], attn_ps[:, :], ring[:, 0, :])]

        names = """wk_loaded wq_loaded wv_loaded wo_loaded x_loaded ctx_head_loaded gates_loaded
            router_loaded rms_loaded w1_loaded w2_loaded
            ident_zero ident_ready causal_zero causal_slots causal_ready slots_zero moe_consts_ready
            ring_filled act_drained dve_drained vector_steps
            ln1_var_ready ln1_rstd_ready xn_ready tanh_ready
            scores_ready scores_read shifted_ready exp_ready probs_ready attn_done x1_ready
            squares_done guard_max_ready guard_rows_ready guard_ready
            warm_ready table_loaded h_base_ready h_scale_ready g_h_scale_ready g_h_ready g_moment_steps ratio_square_ready
            ratio_ready h_ready hT_filled hT_ready hT_full_ready hT_hi_ready rms_filled rms_ready
            logits_filled logits_ready router_exp_ready
            w1_full_ready w1_hi_ready w1_scaled_ready hidden_filled hidden_ready expert_done acc_done last_tile_done result_ready stored
            g_batch_ready g_ctxT_filled g_ctxT_ready g_A_ready
            g_key_filled g_key_ready g_score_filled g_max_ready g_exp_ready g_prob_ready
            g_probT_filled g_probT_ready g_mix_filled g_mix_ready g_out_filled g_vector_steps
            g_stored g_loaded g_x1_ready""".split()
        S = {n: sem(n) for n in names}
        ctx_loaded = [sem(f"ctx_loaded{b}") for b in range(B)]

        def bank_of(job):
            return RING_JOBS.index(job) % RING_BANKS

        def evacuated(job):
            if job in ACT_JOBS:
                return S["act_drained"], ACT_JOBS.index(job) + 1
            return S["dve_drained"], DVE_JOBS.index(job) + 1

        def wait_bank_free(pe, job):
            n = RING_JOBS.index(job)
            if n >= RING_BANKS:
                pe.wait_ge(*evacuated(RING_JOBS[n - RING_BANKS]))

        def wait_filled(eng, job):
            eng.wait_ge(S["ring_filled"], RING_JOBS.index(job) + 1)

        def bank(job, cols=BANK, rows=P):
            return ring[0:rows, bank_of(job), 0:cols]

        def evacuation(job):
            kind = job.rstrip("0123456789.")
            if kind in ("wkT", "wqT", "wvT"):
                dst = {"wkT": wkT, "wqT": wqT, "wvT": wvT}[kind]
                n = int(job[3:])
                return dst[:, 4 * n:4 * n + 4, :], bank(job).rearrange("p (c d) -> p c d", c=4)
            if kind == "ctxT":
                return ctx_headT[:, :], bank(job, B * Q)
            if kind == "xnT":
                return xnT[:, :, 0:Q], bank(job, TOKENS).rearrange("p (b q) -> p b q", b=B)
            if kind in "AM":
                g = int(job[1:])
                dst = {"A": A_T, "M": M}[kind]
                return dst[:, 4 * g:4 * g + 4, :], bank(job).rearrange("p (c d) -> p c d", c=4)
            if kind == "K":
                return keyproj[:, int(job[1:]), :], bank(job, B * Q)
            if kind == "P":
                g = int(job.split(".")[1])
                src = bank(job, rows=Q).rearrange("p (h b s) -> p h b s", h=4, b=2)[:, :, :, 0:Q]
                return probsT[:, 4 * g:4 * g + 4, :].rearrange("p h (b q) -> p h b q", b=2), src
            bb, half = int(job.split(".")[1]), int(job.split(".")[2])
            return (mixT[:, 8 * half:8 * half + 8, bb * Q:bb * Q + Q],
                    bank(job, 8 * Q).rearrange("p (h q) -> p h q", h=8))

        block = ctx.enter_context(nc.Block())

        @block.sync
        def _(sp):
            sp.dma_start(wk[:, :], A["L0_xattn_w_k"]).then_inc(S["wk_loaded"], 16)
            sp.dma_start(wq[:, :], A["L0_xattn_w_q"]).then_inc(S["wq_loaded"], 16)
            sp.dma_start(wo[:, :, :], A["L0_xattn_w_o"].rearrange("(c p) n -> p c n", p=P))\
                .then_inc(S["wo_loaded"], 16)
            sp.wait_ge(S["ring_filled"], RING_JOBS.index("wkT1") + 1)
            sp.dma_start(wv[:, :], A["L0_xattn_w_v"]).then_inc(S["wv_loaded"], 16)
            sp.dma_start(gate_col[:, 0:1], A["g_xattn"].partition_broadcast(P))\
                .then_inc(S["gates_loaded"], 16)
            sp.dma_start(gate_col[:, 1:2], A["g_ffn"].partition_broadcast(P))\
                .then_inc(S["gates_loaded"], 16)
            sp.dma_start(rms_rows[0:SHARED, :], A["L0_ffn_rms_w_s"]).then_inc(S["rms_loaded"], 16)
            sp.dma_start(rms_rows[SHARED:EXPERTS, :], A["L0_ffn_rms_w"])\
                .then_inc(S["rms_loaded"], 16)
            sp.dma_start(router_w[:, :], A["L0_ffn_router_w"]).then_inc(S["router_loaded"], 16)
            for b in range(B):
                sp.dma_start(ctx_all[:, b, :],
                             A["ctx_1024"][b, :, :].rearrange("(p c) d -> p (c d)", c=KC))\
                    .then_inc(ctx_loaded[b], 16)
            sp.dma_start(w1[:, 0:SHARED, :], A["L0_ffn_w1_s"].rearrange("e p f -> p e f"))\
                .then_inc(S["w1_loaded"], 16)
            sp.dma_start(w2[:, 0:SHARED, :, :],
                         A["L0_ffn_w2_s"].rearrange("e (c p) n -> p e c n", p=P))\
                .then_inc(S["w2_loaded"], 16)
            sp.dma_start(w1[:, SHARED:EXPERTS, :], A["L0_ffn_w1"].rearrange("e p f -> p e f"))\
                .then_inc(S["w1_loaded"], 16)
            sp.dma_start(w2[:, SHARED:EXPERTS, :, :],
                         A["L0_ffn_w2"].rearrange("e (c p) n -> p e c n", p=P))\
                .then_inc(S["w2_loaded"], 16)
            out_rows = out.rearrange("b q d -> (b q) d").rearrange("(t p) d -> p t d", p=ROWS)
            for t in range(PAIRS):
                sp.wait_ge(S["result_ready"], t + 1)
                sp.dma_start(out_rows[:, t, :], moe[:, t, :]).then_inc(S["stored"], 16)
            sp.wait_ge(S["stored"], 16 * PAIRS)

        @block.gpsimd
        def _(pool):
            nc.gpsimd.memset(ident[:, :], 0.0).then_inc(S["ident_zero"], 1)
            nc.gpsimd.memset(minus_half[:, :], -0.5)
            pool.wait_ge(S["ident_zero"], 1)
            nc.gpsimd.affine_select(out=ident[:, :], in_=ident[:, :], compare_op=ALU.not_equal,
                                    fill=1.0, base=0, pattern=[[-1, P]], channel_multiplier=1)\
                .then_inc(S["ident_ready"], 1)
            nc.gpsimd.memset(xnT[:, :, :], 0.0).then_inc(S["slots_zero"], 1)
            nc.gpsimd.memset(causal[:, :], 0.0)
            nc.gpsimd.memset(causal_all[:, :, :], 0.0)
            nc.gpsimd.memset(guard_parts[:, :], 0.0).then_inc(S["causal_zero"], 1)
            pool.wait_ge(S["causal_zero"], 1)
            pool.wait_ge(S["ln1_var_ready"], 1)
            nc.gpsimd.tensor_tensor(ln_rstd[:, :], ln_var[:, :], minus_half[:, :], ALU.pow)\
                .then_inc(S["ln1_rstd_ready"], 1)
            pool.wait_ge(S["ln1_rstd_ready"], 1)
            for s in range(2):
                rows = causal[s * SLOT:(s + 1) * SLOT, :]
                nc.gpsimd.affine_select(out=rows, in_=rows, compare_op=ALU.is_ge, fill=MASKED,
                                        base=0, pattern=[[-1, Q]], channel_multiplier=1)\
                    .then_inc(S["causal_slots"], 1)
                pool.wait_ge(S["causal_slots"], s + 1)
            nc.gpsimd.affine_select(out=causal_all[:, :, :], in_=causal_all[:, :, :],
                                    compare_op=ALU.is_ge, fill=MASKED, base=0,
                                    pattern=[[-1, KC], [-KC, 5]], channel_multiplier=1)\
                .then_inc(S["causal_ready"], 1)
            nc.gpsimd.iota(rank[:, :, :], pattern=[[0, PAIRS], [-1, ROUTED]], base=ROUTED,
                           channel_multiplier=0, allow_small_or_imprecise_dtypes=True)
            nc.gpsimd.memset(half[:, :], 0.5).then_inc(S["moe_consts_ready"], 1)

            def scale_w1(slot, e, weights, factors):
                scale = factors.to_broadcast([P, HIDDEN])
                nc.gpsimd.tensor_tensor(w1_full[:, :], weights, scale, ALU.mult)\
                    .then_inc(S["w1_full_ready"], 1)
                nc.gpsimd.tensor_tensor(w1_hi[slot][:, :], weights, scale, ALU.mult)\
                    .then_inc(S["w1_hi_ready"], 1)
                pool.wait_ge(S["w1_hi_ready"], e + 1)
                pool.wait_ge(S["w1_full_ready"], e + 1)
                nc.gpsimd.tensor_tensor(w1_lo[slot][:, :], w1_full[:, :],
                                        w1_hi[slot][:, :].bitcast(FP32), ALU.subtract)\
                    .then_inc(S["w1_scaled_ready"], 1)

            def scale_w1_static(e):
                if e:
                    pool.wait_ge(S["w1_scaled_ready"], e)
                scale_w1(e % 2, e, w1[:, e, :], rms_cols[:, e:e + 1])

            pool.wait_ge(S["rms_ready"], 1)
            pool.wait_ge(S["w1_loaded"], 32)
            for e in range(2):
                scale_w1_static(e)
            pool.wait_ge(S["moe_consts_ready"], 1)
            for t in range(PAIRS):
                pool.wait_ge(S["h_base_ready"], t + 1)
                nc.gpsimd.tensor_tensor(h_scale[:, t:t + 1], h_base[:, t:t + 1],
                                        minus_half[:, 0:1], ALU.pow)\
                    .then_inc(S["h_scale_ready"], 1)
            nc.gpsimd.tensor_tensor(h_scale[:, 0:PAIRS - 1], h_base[:, 0:PAIRS - 1],
                                    minus_half[:, 0:PAIRS - 1], ALU.pow)\
                .then_inc(S["g_h_scale_ready"], 1)
            pool.wait_ge(S["ratio_square_ready"], 1)
            nc.gpsimd.tensor_tensor(ratio[:, :], ratio_square[:, :], half[:, :], ALU.pow)\
                .then_inc(S["ratio_ready"], 1)
            pool.wait_ge(S["hidden_filled"], 1)
            scale_w1_static(2)
            with pool.Fori(0, LOOP_STEPS) as i:
                for u in range(4):
                    e = i * 4 + (LOOP_FROM + u)
                    pool.wait_ge(S["hidden_filled"], e - 1)
                    pool.wait_ge(S["w1_scaled_ready"], e)
                    scale_w1((LOOP_FROM + u) % 2, e,
                             w1[:, bass.ds(e, 1), :].rearrange("p a f -> p (a f)"),
                             rms_cols[:, bass.ds(e, 1)])
            pool.wait_ge(S["hidden_filled"], EXPERTS - 2)
            scale_w1_static(EXPERTS - 1)

        @block.tensor
        def _(pe):
            pe.wait_ge(S["warm_ready"], 1)
            for _n in range(WARM_PRODUCTS):
                nc.tensor.matmul(misc_ps[:, 0:P], warm[:, :], warm[:, :], start=True, stop=True)
            pe.wait_ge(S["ident_ready"], 1)

            def transpose_weights(name, src, n):
                job = f"{name}{n}"
                wait_bank_free(pe, job)
                for i in range(4):
                    c = 4 * n + i
                    last = nc.tensor.transpose(ring[:, bank_of(job), i * P:(i + 1) * P],
                                               src[:, c * P:(c + 1) * P], ident[:, :])
                last.then_inc(S["ring_filled"], 1)

            pe.wait_ge(S["wk_loaded"], 16)
            for n in range(2):
                transpose_weights("wkT", wk, n)
            pe.wait_ge(S["wq_loaded"], 16)
            for n in range(2):
                transpose_weights("wqT", wq, n)

            pe.wait_ge(S["ctx_head_loaded"], 16)
            wait_bank_free(pe, "ctxT")
            for b in range(B):
                last = nc.tensor.transpose(ring[:, bank_of("ctxT"), b * Q:(b + 1) * Q],
                                           ctx_head[:, b, :], ident[0:Q, 0:Q])
            last.then_inc(S["ring_filled"], 1)

            for g in range(GROUPS):
                if g % 2 == 0:
                    pe.wait_ge(*evacuated(f"wkT{g // 2}"))
                    pe.wait_ge(*evacuated(f"wqT{g // 2}"))
                wait_bank_free(pe, f"A{g}")
                r = HEAD * (g % 2)
                for i in range(4):
                    c = head_of(g, i) // 2
                    last = nc.tensor.matmul(ring[:, bank_of(f"A{g}"), i * D:(i + 1) * D],
                                            wkT[r:r + HEAD, c, :], wqT[r:r + HEAD, c, :],
                                            start=True, stop=True)
                last.then_inc(S["ring_filled"], 1)

            def project_keys(s):
                job = f"K{s}"
                if s % 4 == 0:
                    pe.wait_ge(*evacuated(f"A{s // 4}"))
                if s == 0:
                    pe.wait_ge(*evacuated("ctxT"))
                wait_bank_free(pe, job)
                nc.tensor.matmul(ring[:, bank_of(job), 0:B * Q], A_T[:, s, :], ctx_headT[:, :],
                                 start=True, stop=True).then_inc(S["ring_filled"], 1)

            for s in range(4):
                project_keys(s)
            pe.wait_ge(S["xn_ready"], 1)
            wait_bank_free(pe, "xnT")
            for t in range(PAIRS):
                last = nc.tensor.transpose(ring[:, bank_of("xnT"), t * ROWS:(t + 1) * ROWS],
                                           xn_rows[:, t, :], ident[0:ROWS, 0:ROWS])
            last.then_inc(S["ring_filled"], 1)
            for s in range(4, HEADS):
                project_keys(s)

            def scores(t):
                if t == 0:
                    pe.wait_ge(*evacuated("xnT"))
                else:
                    pe.wait_ge(S["scores_read"], 2 * t)
                for half in range(2):
                    if t == 0:
                        pe.wait_ge(*evacuated(f"K{8 * half + 7}"))
                        pe.wait_ge(*evacuated(f"K{8 * half + 6}"))
                    for bb in range(2):
                        b = 2 * t + bb
                        last = nc.tensor.matmul(
                            score_ps[bb * SLOT:(bb + 1) * SLOT, half, 0:8 * Q],
                            xnT[:, b, :], keyproj[:, 8 * half:8 * half + 8, b * Q:(b + 1) * Q],
                            start=True, stop=True)
                    last.then_inc(S["scores_ready"], 1)

            def transpose_probs(t):
                pe.wait_ge(S["probs_ready"], t + 1)
                for g in range(GROUPS):
                    job = f"P{t}.{g}"
                    wait_bank_free(pe, job)
                    for i in range(4):
                        last = nc.tensor.transpose(ring[0:Q, bank_of(job), i * P:(i + 1) * P],
                                                   probs[:, t % 2, 4 * g + i, :], ident[:, :])
                    last.then_inc(S["ring_filled"], 1)

            def mix_context(t):
                for half in range(2):
                    pe.wait_ge(*evacuated(f"P{t}.{2 * half}"))
                    pe.wait_ge(*evacuated(f"P{t}.{2 * half + 1}"))
                    for bb in range(2):
                        job = f"C{t}.{bb}.{half}"
                        wait_bank_free(pe, job)
                        nc.tensor.matmul(ring[:, bank_of(job), 0:8 * Q], ctx_head[:, 2 * t + bb, :],
                                         probsT[:, 8 * half:8 * half + 8, bb * Q:(bb + 1) * Q],
                                         start=True, stop=True).then_inc(S["ring_filled"], 1)

            def attention_out(t):
                if t == 0:
                    pe.wait_ge(*evacuated("M3"))
                    pe.wait_ge(*evacuated("M2"))
                else:
                    pe.wait_ge(S["x1_ready"], t)
                for s in range(HEADS):
                    if s % 8 == 0:
                        for bb in range(2):
                            pe.wait_ge(*evacuated(f"C{t}.{bb}.{s // 8}"))
                    last = nc.tensor.matmul(attn_ps[0:ROWS, 0:D], mixT[:, s, :], M[:, s, :],
                                            start=(s == 0), stop=(s == HEADS - 1))
                last.then_inc(S["attn_done"], 1)

            scores(0)
            pe.wait_ge(S["wv_loaded"], 16)
            for n in range(2):
                transpose_weights("wvT", wv, n)
            pe.wait_ge(S["wo_loaded"], 16)
            for g in range(GROUPS):
                if g % 2 == 0:
                    pe.wait_ge(*evacuated(f"wvT{g // 2}"))
                wait_bank_free(pe, f"M{g}")
                r = HEAD * (g % 2)
                for i in range(4):
                    c = head_of(g, i) // 2
                    last = nc.tensor.matmul(ring[:, bank_of(f"M{g}"), i * D:(i + 1) * D],
                                            wvT[r:r + HEAD, c, :], wo[r:r + HEAD, c, :],
                                            start=True, stop=True)
                last.then_inc(S["ring_filled"], 1)
            pe.wait_ge(S["rms_loaded"], 32)
            nc.tensor.transpose(misc_ps[:, 0:EXPERTS], rms_rows[:, :], ident[0:EXPERTS, 0:EXPERTS])\
                .then_inc(S["rms_filled"], 1)

            for t in range(PAIRS):
                if t + 1 < PAIRS:
                    scores(t + 1)
                transpose_probs(t)
                mix_context(t)
                if t == GUARD_AT:
                    pe.wait_ge(S["guard_max_ready"], 1)
                    pe.wait_ge(S["rms_ready"], 1)
                    for k in range(2):
                        last = nc.tensor.transpose(misc_ps[0:1, k * P:(k + 1) * P],
                                                   guard_max[:, k:k + 1], ident[:, :])
                    last.then_inc(S["guard_rows_ready"], 1)
                if t == PAIRS - 1:
                    pe.wait_ge(S["guard_ready"], 1)
                    ok = pe.value_load(guard_ok[0:1, 0:1], min_val=0, max_val=1)
                attention_out(t)

            with pe.If(ok < 1):
                with pe.Fori(0, B) as b:
                    pe.wait_ge(S["g_batch_ready"], b + 1)
                    for c in range(KC):
                        last = nc.tensor.transpose(ring[:, c // 4, (c % 4) * KP:(c % 4 + 1) * KP],
                                                   g_ctx[:, c, :], ident[0:KP, 0:KP])
                    last.then_inc(S["g_ctxT_filled"], 1)
                    with pe.Fori(0, HEADS) as h:
                        n = b * HEADS + h
                        pe.wait_ge(S["g_ctxT_ready"], b + 1)
                        pe.wait_ge(S["g_A_ready"], n + 1)
                        for k in range(3):
                            last = nc.tensor.matmul(ring[:, k, 0:4 * KP], g_AT[:, :],
                                                    g_ctxT[:, k * 4 * KP:(k + 1) * 4 * KP],
                                                    start=True, stop=True)
                        last.then_inc(S["g_key_filled"], 1)
                        pe.wait_ge(S["g_key_ready"], n + 1)
                        for k in range(3):
                            last = nc.tensor.matmul(ring[0:Q, k, 0:4 * KP], g_xnT[:, :],
                                                    g_key[:, k * 4 * KP:(k + 1) * 4 * KP],
                                                    start=True, stop=True)
                        last.then_inc(S["g_score_filled"], 1)
                        pe.wait_ge(S["g_prob_ready"], n + 1)
                        for c in range(KC):
                            last = nc.tensor.matmul(
                                score_ps[0:KP, c // 8, (c % 8) * Q:(c % 8 + 1) * Q],
                                g_prob[:, c * KP:(c + 1) * KP], ident[0:Q, 0:Q],
                                start=True, stop=True)
                        last.then_inc(S["g_probT_filled"], 1)
                        pe.wait_ge(S["g_probT_ready"], n + 1)
                        for c in range(KC):
                            last = nc.tensor.matmul(attn_ps[:, 0:Q], g_ctx[:, c, :], g_probT[:, c, :],
                                                    start=(c == 0), stop=(c == KC - 1))
                        last.then_inc(S["g_mix_filled"], 1)
                        pe.wait_ge(S["g_mix_ready"], n + 1)
                        nc.tensor.matmul(misc_ps[0:Q, 0:D], g_mixT[:, :],
                                         M[:, bass.ds(h, 1), :].rearrange("p a d -> p (a d)"),
                                         start=True, stop=True).then_inc(S["g_out_filled"], 1)
                pe.wait_ge(S["g_vector_steps"], B * G_BATCH_STEPS)

                pe.wait_ge(S["g_h_ready"], 1)

            def transpose_rows(part):
                tiles, cols, sums = h_parts[part]
                pe.wait_ge(S["h_ready"], tiles[-1] + 1)
                for t in tiles:
                    last = nc.tensor.transpose(sums[:, t * ROWS:(t + 1) * ROWS], h_rows[:, t, :],
                                               ident[0:ROWS, 0:ROWS])
                last.then_inc(S["hT_filled"], 1)

            def router_logits():
                pe.wait_ge(S["router_loaded"], 16)
                pe.wait_ge(S["hT_full_ready"], 2)
                for t in range(PAIRS):
                    last = nc.tensor.matmul(misc_ps[0:ROWS, t * ROUTED:(t + 1) * ROUTED],
                                            hT[:, t * ROWS:(t + 1) * ROWS], router_w[:, :],
                                            start=True, stop=True)
                last.then_inc(S["logits_filled"], 1)

            def hidden_products(slot, cols=slice(0, TOKENS)):
                for c in range(2):
                    hi, lo = (w[slot][:, c * P:(c + 1) * P] for w in (w1_hi, w1_lo))
                    sums = ring[:, 2 * slot + c, cols]
                    nc.tensor.matmul(sums, hi, hT_hi[:, cols], start=True, stop=False)
                    nc.tensor.matmul(sums, hi, hT_lo[:, cols], start=False, stop=False)
                    last = nc.tensor.matmul(sums, lo, hT_hi[:, cols], start=False, stop=True)
                return last

            def output_tile(dst, slot, t, w2_chunk):
                for c in range(2):
                    last = nc.tensor.matmul(dst, hidden[slot][:, c, t * ROWS:(t + 1) * ROWS],
                                            w2_chunk(c), start=(c == 0), stop=(c == 1))
                return last

            def expert_output(slot, w2_chunk):
                for t in range(PAIRS):
                    last = output_tile(score_ps[0:ROWS, slot, t * D:(t + 1) * D], slot, t, w2_chunk)
                last.then_inc(S["expert_done"], 1)

            def static_w2(e):
                return lambda c: w2[:, e, c, :]

            transpose_rows(0)
            for e in range(2):
                pe.wait_ge(S["w1_scaled_ready"], e + 1)
                pe.wait_ge(S["hT_ready"], 1)
                hidden_products(e, h_parts[0][1])
            pe.wait_ge(S["x1_ready"], PAIRS)
            transpose_rows(1)
            pe.wait_ge(S["hT_ready"], 2)
            for e in range(2):
                hidden_products(e, h_parts[1][1]).then_inc(S["hidden_filled"], 1)
            router_logits()
            pe.wait_ge(S["w2_loaded"], 32)
            pe.wait_ge(S["hidden_ready"], 1)
            expert_output(0, static_w2(0))
            pe.wait_ge(S["w1_scaled_ready"], 3)
            hidden_products(0).then_inc(S["hidden_filled"], 1)
            pe.wait_ge(S["hidden_ready"], 2)
            expert_output(1, static_w2(1))
            with pe.Fori(0, LOOP_STEPS) as i:
                for u in range(4):
                    e = i * 4 + (LOOP_FROM + u)
                    slot = (LOOP_FROM + u) % 2
                    pe.wait_ge(S["w1_scaled_ready"], e + 1)
                    pe.wait_ge(S["hidden_ready"], e - 1)
                    hidden_products(slot).then_inc(S["hidden_filled"], 1)
                    pe.wait_ge(S["hidden_ready"], e)
                    pe.wait_ge(S["acc_done"], e - 2)
                    expert_output(1 - slot, lambda c: w2[:, bass.ds(e - 1, 1), c, :]
                                  .rearrange("p a n -> p (a n)"))
            pe.wait_ge(S["w1_scaled_ready"], EXPERTS)
            pe.wait_ge(S["hidden_ready"], EXPERTS - 2)
            hidden_products((EXPERTS - 1) % 2).then_inc(S["hidden_filled"], 1)
            pe.wait_ge(S["hidden_ready"], EXPERTS - 1)
            pe.wait_ge(S["acc_done"], EXPERTS - 3)
            expert_output((EXPERTS - 2) % 2, static_w2(EXPERTS - 2))
            pe.wait_ge(S["hidden_ready"], EXPERTS)
            pe.wait_ge(S["acc_done"], EXPERTS - 2)
            for t in range(PAIRS):
                output_tile(last_tiles[t], (EXPERTS - 1) % 2, t, static_w2(EXPERTS - 1))\
                    .then_inc(S["last_tile_done"], 1)

        @block.scalar
        def _(act):
            act.dma_start(x_rows[:, :, :],
                          A["x"].rearrange("b q d -> (b q) d").rearrange("(t p) d -> p t d", p=ROWS))\
                .then_inc(S["x_loaded"], 16)
            act.dma_start(ctx_head[:, :, :],
                          A["ctx_1024"][:, 0:Q, :].rearrange("b k d -> k b d"))\
                .then_inc(S["ctx_head_loaded"], 16)
            act.wait_ge(S["warm_ready"], 1)
            nc.scalar.activation(tanh_col[0:1, 0:1], warm[0:1, 0:1], ACT.Exp)\
                .then_inc(S["table_loaded"], 1)

            def evacuate_own(jobs):
                for job in jobs:
                    if job in ACT_JOBS:
                        dst, src = evacuation(job)
                        wait_filled(act, job)
                        nc.scalar.activation(dst, src, ACT.Copy).then_inc(S["act_drained"], 1)

            def square_sum(n, column, src):
                if n:
                    act.wait_ge(S["squares_done"], n)
                rows, cols = src.shape[0], src.shape[1]
                nc.scalar.activation(square_junk[0:rows, 0:cols], src, ACT.Square,
                                     accum_out=guard_parts[0:rows, column:column + 1])\
                    .then_inc(S["squares_done"], 1)

            def context_squares(batches):
                for b in batches:
                    act.wait_ge(ctx_loaded[b], 16)
                    square_sum(GROUPS + b, GROUPS + b, ctx_all[:, b, :])

            def softmax_exp(t):
                act.wait_ge(S["shifted_ready"], t + 1)
                nc.scalar.activation(probs[:, t % 2, :, :], probs[:, t % 2, :, :], ACT.Exp)\
                    .then_inc(S["exp_ready"], 1)

            cut = [RING_JOBS.index(j) for j in ("K8", "wvT0", "P0.0")]
            evacuate_own(RING_JOBS[:cut[0]])
            act.wait_ge(S["causal_zero"], 1)
            for g in range(GROUPS):
                act.wait_ge(*evacuated(f"A{g}"))
                square_sum(g, g, A_T[:, 4 * g:4 * g + 4, :].rearrange("p h d -> p (h d)"))
            evacuate_own(RING_JOBS[cut[0]:cut[1]])
            evacuate_own(RING_JOBS[cut[1]:cut[2]])
            context_squares(range(0, 1))
            act.wait_ge(S["gates_loaded"], 32)
            act.wait_ge(S["table_loaded"], 1)
            nc.scalar.activation(tanh_col[:, :], gate_col[:, :], ACT.Tanh).then_inc(S["tanh_ready"], 1)
            softmax_exp(0)
            for t in range(PAIRS):
                evacuate_own([f"P{t}.{g}" for g in range(GROUPS)])
                if t + 1 < PAIRS:
                    softmax_exp(t + 1)
                evacuate_own([f"C{t}.{bb}.{half}" for half in range(2) for bb in range(2)])
                context_squares([range(1, 4), range(4, 8), [], []][t])

            act.wait_ge(S["guard_ready"], 1)
            ok = act.value_load(guard_ok[0:1, 0:1], min_val=0, max_val=1)
            with act.If(ok < 1):
                with act.Fori(0, B) as b:
                    act.wait_ge(S["g_ctxT_filled"], b + 1)
                    nc.scalar.activation(g_ctxT.rearrange("p (k n) -> p k n", k=3),
                                         ring[:, 0:3, 0:4 * KP], ACT.Copy)\
                        .then_inc(S["g_ctxT_ready"], 1)
                    with act.Fori(0, HEADS) as h:
                        n = b * HEADS + h
                        act.wait_ge(S["g_key_filled"], n + 1)
                        nc.scalar.activation(g_key.rearrange("p (k n) -> p k n", k=3),
                                             ring[:, 0:3, 0:4 * KP], ACT.Copy)\
                            .then_inc(S["g_key_ready"], 1)
                        act.wait_ge(S["g_max_ready"], n + 1)
                        nc.scalar.activation(g_prob, g_prob, ACT.Exp, bias=g_max[:, 0:1],
                                             accum_out=g_sum[:, 0:1]).then_inc(S["g_exp_ready"], 1)
                        act.wait_ge(S["g_probT_filled"], n + 1)
                        nc.scalar.activation(g_probT[:, 0:8, :].rearrange("p c q -> p (c q)"),
                                             score_ps[0:KP, 0, 0:8 * Q], ACT.Copy)
                        nc.scalar.activation(g_probT[:, 8:KC, :].rearrange("p c q -> p (c q)"),
                                             score_ps[0:KP, 1, 0:(KC - 8) * Q], ACT.Copy)\
                            .then_inc(S["g_probT_ready"], 1)
                        act.wait_ge(S["g_mix_filled"], n + 1)
                        nc.scalar.activation(g_mixT[:, :], attn_ps[:, 0:Q], ACT.Copy)\
                            .then_inc(S["g_mix_ready"], 1)
                    act.wait_ge(S["g_vector_steps"], (b + 1) * G_BATCH_STEPS)
                    act.dma_start(g_attn_dram[bass.ds(b * Q, Q), :], g_acc[:, :])\
                        .then_inc(S["g_stored"], 16)
                act.wait_ge(S["g_stored"], 16 * B)
                act.dma_start(attn_all[:, :, :], g_attn_dram.rearrange("(t p) d -> p t d", p=ROWS))\
                    .then_inc(S["g_loaded"], 16)
                act.wait_ge(S["g_loaded"], 16)

            for part, (_tiles, cols, sums) in enumerate(h_parts):
                act.wait_ge(S["hT_filled"], part + 1)
                nc.scalar.activation(hT_hi[:, cols], sums[:, cols], ACT.Copy)\
                    .then_inc(S["hT_hi_ready"], 1)
            for part, (_tiles, cols, sums) in enumerate(h_parts):
                act.wait_ge(S["hT_ready"], part + 1)
                nc.scalar.activation(hT[:, cols], sums[:, cols], ACT.Copy)\
                    .then_inc(S["hT_full_ready"], 1)
            act.wait_ge(S["logits_ready"], 1)
            nc.scalar.activation(expo[:, :, :], shifted[:, :, :], ACT.Exp)\
                .then_inc(S["router_exp_ready"], 1)

            def silu(slot):
                nc.scalar.activation(hidden[slot], ring[:, 2 * slot:2 * slot + 2, 0:TOKENS],
                                     ACT.Silu).then_inc(S["hidden_ready"], 1)

            for e in range(LOOP_FROM):
                act.wait_ge(S["hidden_filled"], e + 1)
                if e >= 2:
                    act.wait_ge(S["expert_done"], e - 1)
                silu(e % 2)
            with act.Fori(0, LOOP_STEPS) as i:
                for u in range(4):
                    e = i * 4 + (LOOP_FROM + u)
                    act.wait_ge(S["hidden_filled"], e + 1)
                    act.wait_ge(S["expert_done"], e - 1)
                    silu((LOOP_FROM + u) % 2)
            act.wait_ge(S["hidden_filled"], EXPERTS)
            act.wait_ge(S["expert_done"], EXPERTS - 2)
            silu((EXPERTS - 1) % 2)

        @block.vector
        def _(dve):
            steps = [0]

            def then_wait(instruction):
                steps[0] += 1
                instruction.then_inc(S["vector_steps"], 1)
                dve.wait_ge(S["vector_steps"], steps[0])

            def evacuate_own(jobs):
                for job in jobs:
                    if job in DVE_JOBS:
                        dst, src = evacuation(job)
                        wait_filled(dve, job)
                        nc.vector.tensor_copy(dst, src).then_inc(S["dve_drained"], 1)

            def moments(rows):
                for t in range(PAIRS):
                    last = nc.vector.bn_stats(ln_stats[:, t, :], rows[:, t, :])
                then_wait(last)
                for t in range(PAIRS):
                    last = nc.vector.bn_aggr(ln_mv[:, t, :], ln_stats[:, t, :])
                then_wait(last)

            nc.vector.memset(warm[:, :], 0.0).then_inc(S["warm_ready"], 1)
            dve.wait_ge(S["x_loaded"], 16)
            moments(x_rows)
            nc.vector.tensor_scalar(ln_var[:, :], ln_mv[:, :, 1], LN_EPS, None, ALU.add)\
                .then_inc(S["ln1_var_ready"], 1)
            cut = [RING_JOBS.index(j) for j in ("K0", "wvT0", "P0.0")]
            evacuate_own(RING_JOBS[:cut[0]])
            dve.wait_ge(S["ln1_rstd_ready"], 1)
            for t in range(PAIRS):
                last = nc.vector.tensor_scalar(xn_rows[:, t, :], x_rows[:, t, :], ln_mv[:, t, 0:1],
                                               ln_rstd[:, t:t + 1], ALU.subtract, ALU.mult)
            last.then_inc(S["xn_ready"], 1)
            dve.wait_ge(S["slots_zero"], 1)
            evacuate_own(RING_JOBS[cut[0]:cut[1]])
            dve.wait_ge(S["causal_ready"], 1)

            def softmax_shift(t):
                p = probs[:, t % 2, :, :]
                if t >= 2:
                    dve.wait_ge(S["ring_filled"], RING_JOBS.index(f"P{t - 2}.{GROUPS - 1}") + 1)
                for half in range(2):
                    dve.wait_ge(S["scores_ready"], 2 * t + half + 1)
                    nc.vector.scalar_tensor_tensor(
                        out=probs[:, t % 2, 8 * half:8 * half + 8, :],
                        in0=score_ps[:, half, 0:8 * Q].rearrange("p (h k) -> p h k", h=8),
                        scalar=SCALE, in1=causal[:, :].unsqueeze(1).to_broadcast([P, 8, Q]),
                        op0=ALU.mult, op1=ALU.add).then_inc(S["scores_read"], 1)
                dve.wait_ge(S["scores_read"], 2 * t + 2)
                then_wait(nc.vector.tensor_reduce(row_max[:, :], p, AX.X, ALU.max))
                nc.vector.tensor_tensor(p, p, row_max[:, :].unsqueeze(2).to_broadcast([P, HEADS, Q]),
                                        ALU.subtract).then_inc(S["shifted_ready"], 1)

            def softmax_normalise(t):
                p = probs[:, t % 2, :, :]
                dve.wait_ge(S["exp_ready"], t + 1)
                then_wait(nc.vector.tensor_reduce(row_sum[:, :], p, AX.X, ALU.add))
                then_wait(nc.vector.reciprocal(row_inv[:, :], row_sum[:, :]))
                nc.vector.tensor_tensor(p, p, row_inv[:, :].unsqueeze(2).to_broadcast([P, HEADS, Q]),
                                        ALU.mult).then_inc(S["probs_ready"], 1)

            def first_residual(t):
                dve.wait_ge(S["attn_done"], t + 1)
                nc.vector.scalar_tensor_tensor(out=x1[:, t, :], in0=attn_ps[0:ROWS, 0:D],
                                               scalar=tanh_col[0:ROWS, 0:1], in1=x_rows[:, t, :],
                                               op0=ALU.mult, op1=ALU.add)\
                    .then_inc(S["x1_ready"], 1)

            def second_moments(tiles, after_step=then_wait):
                for t in tiles:
                    last = nc.vector.bn_stats(ln_stats[:, t, :], x1[:, t, :])
                after_step(last)
                for t in tiles:
                    last = nc.vector.bn_aggr(ln_mv[:, t, :], ln_stats[:, t, :])
                after_step(last)
                cols = slice(tiles[0], tiles[-1] + 1)
                return nc.vector.tensor_scalar(h_base[:, cols], ln_mv[:, cols, 1],
                                               1.0 + RMS_EPS, LN_EPS * RMS_EPS, ALU.mult, ALU.add)

            def normalised(t):
                return nc.vector.tensor_scalar(h_rows[:, t, :], x1[:, t, :], ln_mv[:, t, 0:1],
                                               h_scale[:, t:t + 1], ALU.subtract, ALU.mult)

            softmax_shift(0)
            evacuate_own(RING_JOBS[cut[1]:cut[2]])
            softmax_normalise(0)
            dve.wait_ge(S["rms_filled"], 1)
            nc.vector.tensor_copy(rms_cols[:, :], misc_ps[:, 0:EXPERTS]).then_inc(S["rms_ready"], 1)
            dve.wait_ge(S["tanh_ready"], 1)
            nc.vector.tensor_copy(gates[:, 0:SHARED, :], tanh_col[0:ROWS, 1:2].unsqueeze(2)
                                  .to_broadcast([ROWS, SHARED, PAIRS]))
            for t in range(PAIRS):
                if t + 1 < PAIRS:
                    softmax_shift(t + 1)
                    softmax_normalise(t + 1)
                if t == GUARD_AT:
                    dve.wait_ge(S["squares_done"], GROUPS + B)
                    nc.vector.tensor_reduce(guard_max[:, 0:1], guard_parts[:, 0:GROUPS], AX.X, ALU.max)
                    nc.vector.tensor_reduce(guard_max[:, 1:2], guard_parts[:, GROUPS:GROUPS + B],
                                            AX.X, ALU.max).then_inc(S["guard_max_ready"], 1)
                if t >= 1:
                    dve.wait_ge(S["h_scale_ready"], t)
                    normalised(t - 1).then_inc(S["h_ready"], 1)
                if t == GUARD_AT:
                    dve.wait_ge(S["guard_rows_ready"], 1)
                    then_wait(nc.vector.tensor_reduce(
                        guard_pair[:, :], misc_ps[0:1, 0:2 * P].rearrange("p (k n) -> p k n", k=2),
                        AX.X, ALU.max))
                    then_wait(nc.vector.tensor_tensor(guard_prod[:, :], guard_pair[:, 0:1],
                                                      guard_pair[:, 1:2], ALU.mult))
                    nc.vector.tensor_scalar(guard_ok[:, :], guard_prod[:, :], GUARD_LIMIT, None,
                                            ALU.is_lt).then_inc(S["guard_ready"], 1)
                if t == PAIRS - 1:
                    dve.wait_ge(S["guard_ready"], 1)
                    ok = dve.value_load(guard_ok[0:1, 0:1], min_val=0, max_val=1)
                first_residual(t)
                if t < PAIRS - 1:
                    dve.wait_ge(S["x1_ready"], t + 1)
                    second_moments([t]).then_inc(S["h_base_ready"], 1)

            with dve.If(ok < 1):
                with dve.Fori(0, B) as b:
                    nc.vector.memset(g_acc[:, :], 0.0).then_inc(S["g_vector_steps"], 1)
                    nc.vector.tensor_copy(g_xnT[:, :], xnT[:, bass.ds(b, 1), 0:Q]
                                          .rearrange("p a q -> p (a q)"))
                    nc.vector.tensor_copy(g_ctx.rearrange("p c d -> p (c d)"),
                                          ctx_all[:, bass.ds(b, 1), :].rearrange("p a n -> p (a n)"))\
                        .then_inc(S["g_batch_ready"], 1)
                    with dve.Fori(0, HEADS) as h:
                        n = b * HEADS + h
                        done = b * G_BATCH_STEPS + h * G_HEAD_STEPS + 1
                        nc.vector.tensor_copy(g_AT[:, :], A_T[:, bass.ds(h, 1), :]
                                              .rearrange("p a d -> p (a d)"))\
                            .then_inc(S["g_A_ready"], 1)
                        dve.wait_ge(S["g_score_filled"], n + 1)
                        nc.vector.tensor_scalar(g_prob.rearrange("p (k n) -> p k n", k=3),
                                                ring[0:Q, 0:3, 0:4 * KP], SCALE, MASKED,
                                                ALU.mult, ALU.add).then_inc(S["g_vector_steps"], 1)
                        dve.wait_ge(S["g_vector_steps"], done + 1)
                        for k in range(3):
                            src = ring[0:Q, k, 0:4 * KP].rearrange("p (c n) -> p c n", c=4)
                            dst = g_prob[:, k * 4 * KP:(k + 1) * 4 * KP]
                            last = nc.vector.scalar_tensor_tensor(
                                out=dst.rearrange("p (c n) -> p c n", c=4)[:, :, 0:5],
                                in0=src[:, :, 0:5], scalar=SCALE,
                                in1=causal_all[:, 4 * k:4 * k + 4, :], op0=ALU.mult, op1=ALU.add)
                        last.then_inc(S["g_vector_steps"], 1)
                        dve.wait_ge(S["g_vector_steps"], done + 2)
                        nc.vector.tensor_reduce(g_max[:, :], g_prob, AX.X, ALU.max, negate=True)\
                            .then_inc(S["g_max_ready"], 1)
                        dve.wait_ge(S["g_exp_ready"], n + 1)
                        nc.vector.reciprocal(g_inv[:, :], g_sum[:, :])\
                            .then_inc(S["g_vector_steps"], 1)
                        dve.wait_ge(S["g_vector_steps"], done + 3)
                        nc.vector.tensor_scalar(g_prob, g_prob, g_inv[:, 0:1], None, ALU.mult)\
                            .then_inc(S["g_prob_ready"], 1)
                        dve.wait_ge(S["g_out_filled"], n + 1)
                        nc.vector.tensor_tensor(g_acc[:, :], g_acc[:, :], misc_ps[0:Q, 0:D], ALU.add)\
                            .then_inc(S["g_vector_steps"], 1)
                    dve.wait_ge(S["g_stored"], (b + 1) * 16)
                dve.wait_ge(S["g_loaded"], 16)
                for t in range(PAIRS):
                    last = nc.vector.scalar_tensor_tensor(
                        out=x1[:, t, :], in0=attn_all[:, t, :], scalar=tanh_col[0:ROWS, 0:1],
                        in1=x_rows[:, t, :], op0=ALU.mult, op1=ALU.add)
                last.then_inc(S["g_x1_ready"], 1)
                dve.wait_ge(S["g_x1_ready"], 1)
                g_steps = [0]

                def g_then_wait(instruction):
                    g_steps[0] += 1
                    instruction.then_inc(S["g_moment_steps"], 1)
                    dve.wait_ge(S["g_moment_steps"], g_steps[0])

                second_moments(range(PAIRS - 1), g_then_wait)

            def subtract_hi(part):
                _tiles, cols, sums = h_parts[part]
                dve.wait_ge(S["hT_hi_ready"], part + 1)
                nc.vector.tensor_tensor(hT_lo[:, cols], sums[:, cols], hT_hi[:, cols].bitcast(FP32),
                                        ALU.subtract).then_inc(S["hT_ready"], 1)

            dve.wait_ge(S["x1_ready"], PAIRS)
            second_moments([PAIRS - 1]).then_inc(S["h_base_ready"], 1)
            with dve.If(ok < 1):
                dve.wait_ge(S["g_h_scale_ready"], 1)
                for t in range(PAIRS - 1):
                    last = normalised(t)
                last.then_inc(S["g_h_ready"], 1)
            subtract_hi(0)
            dve.wait_ge(S["h_scale_ready"], PAIRS)
            normalised(PAIRS - 1).then_inc(S["h_ready"], 1)

            then_wait(nc.vector.tensor_scalar(ln2_var[:, :], ln_mv[:, :, 1], LN_EPS, None, ALU.add))
            then_wait(nc.vector.reciprocal(ln2_inv[:, :], ln2_var[:, :]))
            nc.vector.tensor_tensor(ratio_square[:, :], h_base[:, :], ln2_inv[:, :], ALU.mult)\
                .then_inc(S["ratio_square_ready"], 1)
            subtract_hi(1)

            def wide(col):
                return col[:, :].unsqueeze(2).to_broadcast([ROWS, PAIRS, ROUTED])

            dve.wait_ge(S["logits_filled"], 1)
            dve.wait_ge(S["ratio_ready"], 1)
            then_wait(nc.vector.tensor_tensor(
                logits[:, :, :],
                misc_ps[0:ROWS, 0:PAIRS * ROUTED].rearrange("p (t e) -> p t e", t=PAIRS),
                wide(ratio), ALU.mult))
            then_wait(nc.vector.tensor_reduce(logit_max[:, :], logits[:, :, :], AX.X, ALU.max))
            nc.vector.tensor_tensor(shifted[:, :, :], logits[:, :, :], wide(logit_max), ALU.subtract)\
                .then_inc(S["logits_ready"], 1)
            dve.wait_ge(S["router_exp_ready"], 1)
            dve.wait_ge(S["moe_consts_ready"], 1)
            nc.vector.tensor_reduce(exp_sum[:, :], expo[:, :, :], AX.X, ALU.add)
            for i, values in enumerate((expo, rest)):
                then_wait(nc.vector.tensor_reduce(top[i][:, :], values[:, :, :], AX.X, ALU.max))
                then_wait(nc.vector.tensor_tensor(hit[i][:, :, :], values[:, :, :], wide(top[i]),
                                                  ALU.is_ge))
                then_wait(nc.vector.tensor_tensor(tie[i][:, :, :], hit[i][:, :, :], rank[:, :, :],
                                                  ALU.mult))
                then_wait(nc.vector.tensor_reduce(best_rank[i][:, :], tie[i][:, :, :], AX.X, ALU.max))
                then_wait(nc.vector.tensor_tensor(pick[i][:, :, :], tie[i][:, :, :],
                                                  wide(best_rank[i]), ALU.is_equal))
                if i == 0:
                    then_wait(nc.vector.scalar_tensor_tensor(
                        out=rest[:, :, :], in0=pick[0][:, :, :], scalar=-2.0, in1=expo[:, :, :],
                        op0=ALU.mult, op1=ALU.add))
            then_wait(nc.vector.tensor_tensor(pick[0][:, :, :], pick[0][:, :, :], pick[1][:, :, :],
                                              ALU.add))
            then_wait(nc.vector.tensor_tensor(chosen[:, :, :], pick[0][:, :, :], expo[:, :, :],
                                              ALU.mult))
            then_wait(nc.vector.tensor_reduce(top_sum[:, :], chosen[:, :, :], AX.X, ALU.add))
            then_wait(nc.vector.scalar_tensor_tensor(out=gate_den[:, :], in0=exp_sum[:, :],
                                                     scalar=GATE_EPS, in1=top_sum[:, :],
                                                     op0=ALU.mult, op1=ALU.add))
            then_wait(nc.vector.reciprocal(gate_inv[:, :], gate_den[:, :]))
            then_wait(nc.vector.tensor_scalar(gate_inv[:, :], gate_inv[:, :],
                                              tanh_col[0:ROWS, 1:2], None, ALU.mult))
            then_wait(nc.vector.tensor_tensor(
                gates[:, SHARED:EXPERTS, :].rearrange("p e t -> p t e"), chosen[:, :, :],
                wide(gate_inv), ALU.mult))

            def add_expert(slot, gate, before=moe):
                for t in range(PAIRS):
                    last = nc.vector.scalar_tensor_tensor(
                        out=moe[:, t, :], in0=score_ps[0:ROWS, slot, t * D:(t + 1) * D],
                        scalar=gate(t), in1=before[:, t, :], op0=ALU.mult, op1=ALU.add)
                last.then_inc(S["acc_done"], 1)

            def static_gate(e):
                return lambda t: gates[:, e, t:t + 1]

            dve.wait_ge(S["expert_done"], 1)
            add_expert(0, static_gate(0), before=x1)
            for e in range(1, LOOP_FROM):
                dve.wait_ge(S["expert_done"], e + 1)
                dve.wait_ge(S["acc_done"], e)
                add_expert(e % 2, static_gate(e))
            with dve.Fori(0, LOOP_STEPS) as i:
                for u in range(4):
                    e = i * 4 + (LOOP_FROM + u)
                    dve.wait_ge(S["expert_done"], e + 1)
                    dve.wait_ge(S["acc_done"], e)
                    add_expert((LOOP_FROM + u) % 2, lambda t: gates[:, bass.ds(e, 1), t]
                               .rearrange("p a -> p a"))
            dve.wait_ge(S["acc_done"], EXPERTS - 1)
            e = EXPERTS - 1
            for t in range(PAIRS):
                dve.wait_ge(S["last_tile_done"], t + 1)
                nc.vector.scalar_tensor_tensor(
                    out=moe[:, t, :], in0=last_tiles[t],
                    scalar=gates[:, e, t:t + 1], in1=moe[:, t, :], op0=ALU.mult, op1=ALU.add)\
                    .then_inc(S["result_ready"], 1)


_INS = ["x", "ctx_1024", "g_xattn", "g_ffn", "L0_xattn_w_q", "L0_xattn_w_k", "L0_xattn_w_v",
        "L0_xattn_w_o", "L0_ffn_router_w", "L0_ffn_rms_w", "L0_ffn_w1", "L0_ffn_w2",
        "L0_ffn_rms_w_s", "L0_ffn_w1_s", "L0_ffn_w2_s"]


def kernel(**inputs):
    import numpy as _np
    import concourse.bacc as _bacc
    from concourse import mybir as _mybir
    from concourse.bass_utils import run_bass_kernel_spmd as _run

    nc = _bacc.Bacc("TRN2", target_bir_lowering=False, num_devices=1)
    arrays, args = {}, {}
    for name in _INS:
        a = _np.ascontiguousarray(inputs[name])
        arrays[f"in_{name}_dram"] = a
        args[name] = nc.dram_tensor(f"in_{name}_dram", a.shape, _mybir.dt.from_np(a.dtype),
                                    kind="ExternalInput").ap()
    out = nc.dram_tensor("out_0_dram", (B, Q, D), _mybir.dt.float32, kind="ExternalOutput").ap()
    build(nc, args, out)
    r = _run(nc, [arrays], core_ids=[0])
    return r.results[0]["out_0_dram"]
```

```python
from contextlib import ExitStack

import concourse.bass as bass
from concourse import mybir

FP32 = mybir.dt.float32
FP32R = mybir.dt.float32r
BF16 = mybir.dt.bfloat16
INT32 = mybir.dt.int32
ACT = mybir.ActivationFunctionType
ALU = mybir.AluOpType
AX = mybir.AxisListType

B, Q, D = 8, 56, 128
KEYS = 1500
HEADS, HEAD = 16, 64
INNER = HEADS * HEAD
ROUTED, SHARED, HIDDEN = 14, 2, 256
EXPERTS = ROUTED + SHARED
TOKENS = B * Q
P = 128
PAIRS = B // 2
ROWS = 2 * Q
SLOT = 64
BANK = 512
KC = 12
KP = KEYS // KC
CHUNKS = INNER // P
GROUPS = HEADS // 4

SCALE = HEAD ** -0.5
MASKED = -10000.0
LN_EPS = 1e-5
RMS_EPS = 1.1920929e-07
GATE_EPS = 1e-9

SCORE_LIMIT = 4900.0
GUARD_LIMIT = SCORE_LIMIT ** 2 / (SCALE ** 2 * D * P)


def head_of(group, i):
    return 8 * (group // 2) + 2 * i + group % 2


RING_JOBS = (
    ["wkT0", "wkT1", "wqT0", "wqT1", "ctxT"]
    + [f"A{g}" for g in range(GROUPS)]
    + [f"K{s}" for s in range(6)] + ["xnT"] + [f"K{s}" for s in range(6, HEADS)]
    + ["wvT0", "wvT1"] + [f"M{g}" for g in range(GROUPS)]
)
for _t in range(PAIRS):
    RING_JOBS += [f"P{_t}.{g}" for g in range(GROUPS)]
    RING_JOBS += [f"C{_t}.{bb}.{half}" for half in range(2) for bb in range(2)]
RING_BANKS = 4
WARM_PRODUCTS = 31
SPLIT_PRODUCTS = 10
LOOP_FROM = 3
LOOP_STEPS = (EXPERTS - LOOP_FROM - 1) // 4
G_HEAD_STEPS = 4
G_BATCH_STEPS = 1 + HEADS * G_HEAD_STEPS
SPLIT_JOBS = [j for j in RING_JOBS if j == "ctxT" or j[0] in "AP"]
ACT_JOBS = [j for j in RING_JOBS if j in SPLIT_JOBS or j[0] == "C" or j[:3] == "wvT"
            or (j != "xnT" and int(j.lstrip("wkqTKM")) % 2 == 0)]
DVE_JOBS = [j for j in RING_JOBS if j in SPLIT_JOBS or j not in ACT_JOBS]
STACK = SLOT + Q


def build(nc, A, out):
    ctx = ExitStack()
    with ctx:
        def sb(name, shape, dt=FP32):
            return ctx.enter_context(nc.sbuf_tensor(name, shape, dt))

        def pb(name, shape, dt=FP32):
            return ctx.enter_context(nc.psum_tensor(name, shape, dt))

        def sem(name):
            return ctx.enter_context(nc.semaphore(name))

        wq_space = sb("wq_space", [P, 2 * INNER])
        wq = wq_space[:, 0:INNER]
        wk = sb("wk", [P, INNER])
        wv = wk
        wo = sb("wo", [P, CHUNKS, D])
        wqT = wq_space[:, INNER:2 * INNER].rearrange("p (c d) -> p c d", c=CHUNKS)
        wkT = sb("wkT", [P, CHUNKS, D])
        wvT = wkT
        A_hi = sb("A_hi", [P, HEADS, D], FP32R)
        A_lo = sb("A_lo", [P, HEADS, D], FP32R)
        M = wq_space[:, :].rearrange("p (h d) -> p h d", h=HEADS)
        x_space = sb("x_space", [P, PAIRS * D])
        x_rows = x_space[0:ROWS, :].rearrange("p (t d) -> p t d", t=PAIRS)
        xn_rows = sb("xn_rows", [ROWS, PAIRS, D])
        xnT = sb("xnT", [P, B, SLOT])
        ctx_head = sb("ctx_head", [Q, B, D])
        ctx_headT_hi = sb("ctx_headT_hi", [P, B * Q], FP32R)
        ctx_headT_lo = sb("ctx_headT_lo", [P, B * Q], FP32R)
        ctx_stack = sb("ctx_stack", [STACK, B, D], FP32R)
        ctx_lo = sb("ctx_lo", [Q, B, D], FP32R)
        ctx_all = sb("ctx_all", [KP, B, KC * D])
        keyproj = sb("keyproj", [P, HEADS, B * Q])
        probs = sb("probs", [P, 2, HEADS, Q])
        probs_stack = sb("probs_stack", [STACK, HEADS, ROWS], FP32R)
        mixT = sb("mixT", [P, HEADS, ROWS])
        hidden_slots = mixT[:, :, :].rearrange("p h n -> p (h n)")\
            .rearrange("p (s c n) -> p s c n", s=2, c=2)
        hidden = [hidden_slots[:, s, :, :] for s in range(2)]
        square_junk = sb("square_junk", [P, KC * D], BF16)
        ident = sb("ident", [P, P])
        mask_full = sb("mask_full", [P, Q])
        mask = sb("mask", [P, Q], FP32R)
        ident_r = sb("ident_r", [P, P], FP32R)
        causal_all = sb("causal_all", [Q, KC, 5])
        row_max = sb("row_max", [P, HEADS])
        row_sum = sb("row_sum", [P, HEADS])
        row_inv = sb("row_inv", [P, HEADS])
        ln_stats = sb("ln_stats", [ROWS, PAIRS, 6])
        ln_mv = sb("ln_mv", [ROWS, PAIRS, 2])
        ln_var = sb("ln_var", [ROWS, PAIRS])
        ln_rstd = sb("ln_rstd", [ROWS, PAIRS])
        minus_half = sb("minus_half", [ROWS, PAIRS])
        gate_col = sb("gate_col", [P, 2])
        tanh_col = sb("tanh_col", [P, 2])
        guard_parts = sb("guard_parts", [P, GROUPS + B])
        guard_max = sb("guard_max", [P, 2])
        guard_pair = sb("guard_pair", [1, 2])
        guard_prod = sb("guard_prod", [1, 1])
        guard_ok = sb("guard_ok", [1, 1], INT32)
        x1 = sb("x1", [ROWS, PAIRS, D])
        router_w = sb("router_w", [P, ROUTED])
        rms_rows = sb("rms_rows", [EXPERTS, D])
        rms_cols = sb("rms_cols", [P, EXPERTS])
        w1 = sb("w1", [P, EXPERTS, HIDDEN])
        w2 = sb("w2", [P, EXPERTS, 2, D])
        w1_full = sb("w1_full", [P, HIDDEN])
        w1_hi = [sb(f"w1_hi{s}", [P, HIDDEN], FP32R) for s in range(2)]
        w1_lo = [sb(f"w1_lo{s}", [P, HIDDEN], FP32R) for s in range(2)]
        h_base = sb("h_base", [ROWS, PAIRS])
        h_scale = sb("h_scale", [ROWS, PAIRS])
        ln2_var = sb("ln2_var", [ROWS, PAIRS])
        ln2_inv = sb("ln2_inv", [ROWS, PAIRS])
        ratio_square = sb("ratio_square", [ROWS, PAIRS])
        plus_half = sb("plus_half", [ROWS, PAIRS])
        table_probe = sb("table_probe", [1, 1])
        warm = sb("warm", [P, P], BF16)
        ratio = sb("ratio", [ROWS, PAIRS])
        h_rows = xn_rows
        hT = x_space[:, 0:TOKENS]
        hT_hi = sb("hT_hi", [P, TOKENS], FP32R)
        hT_lo = sb("hT_lo", [P, TOKENS], FP32R)
        logits = sb("logits", [ROWS, PAIRS, ROUTED])
        shifted = sb("shifted", [ROWS, PAIRS, ROUTED])
        expo = sb("expo", [ROWS, PAIRS, ROUTED])
        rank = sb("rank", [ROWS, PAIRS, ROUTED])
        hit = [sb(f"hit{i}", [ROWS, PAIRS, ROUTED]) for i in range(2)]
        tie = [sb(f"tie{i}", [ROWS, PAIRS, ROUTED]) for i in range(2)]
        pick = [sb(f"pick{i}", [ROWS, PAIRS, ROUTED]) for i in range(2)]
        rest = sb("rest", [ROWS, PAIRS, ROUTED])
        chosen = sb("chosen", [ROWS, PAIRS, ROUTED])
        top = [sb(f"top{i}", [ROWS, PAIRS]) for i in range(2)]
        best_rank = [sb(f"best_rank{i}", [ROWS, PAIRS]) for i in range(2)]
        logit_max = sb("logit_max", [ROWS, PAIRS])
        exp_sum = sb("exp_sum", [ROWS, PAIRS])
        top_sum = sb("top_sum", [ROWS, PAIRS])
        gate_den = sb("gate_den", [ROWS, PAIRS])
        gate_inv = sb("gate_inv", [ROWS, PAIRS])
        gates = sb("gates", [ROWS, EXPERTS, PAIRS])
        moe = h_rows

        def lay(space, at, rows, n):
            return space[0:rows, at:at + n]

        key_space = keyproj[:, :, :].rearrange("p h n -> p (h n)")
        prob_space = probs[:, :, :, :].rearrange("p s h k -> p (s h k)")
        mix_space = mixT[:, :, :].rearrange("p h n -> p (h n)")
        g_ctx = lay(key_space, 0, KP, KC * D).rearrange("p (c d) -> p c d", c=KC)
        g_ctxT = lay(key_space, 1536, P, KEYS)
        g_key = lay(key_space, 3072, P, KEYS)
        g_prob = lay(key_space, 4608, Q, KEYS)
        g_probT = lay(key_space, 6144, KP, KC * Q).rearrange("p (c q) -> p c q", c=KC)
        g_xnT = lay(prob_space, 0, P, Q)
        g_AT = lay(prob_space, 128, P, D)
        g_mixT = lay(prob_space, 256, P, Q)
        g_acc = lay(prob_space, 384, Q, D)
        attn_all = lay(mix_space, 0, ROWS, PAIRS * D).rearrange("p (t d) -> p t d", t=PAIRS)
        g_max = sb("g_max", [Q, 1])
        g_sum = sb("g_sum", [Q, 1])
        g_inv = sb("g_inv", [Q, 1])
        g_attn_dram = nc.dram_tensor("g_attn_dram", [TOKENS, D], FP32, kind="Internal").ap()

        ring = pb("ring", [P, RING_BANKS, BANK])
        score_ps = pb("score_ps", [P, 2, BANK])
        attn_ps = pb("attn_ps", [P, BANK])
        misc_ps = pb("misc_ps", [P, BANK])

        first_tiles = (PAIRS - 1) * ROWS
        h_parts = [(range(PAIRS - 1), slice(0, first_tiles), misc_ps),
                   ([PAIRS - 1], slice(first_tiles, TOKENS), attn_ps)]

        def logit_col(t):
            return first_tiles + t * ROUTED

        last_tiles = [bank_tile[0:ROWS, 0:D] for bank_tile in
                      (score_ps[:, 0, :], misc_ps[:, :], attn_ps[:, :], ring[:, 0, :],
                       score_ps[:, 1, :], ring[:, 1, :], ring[:, 2, :], ring[:, 3, :])]

        names = """wv_loaded wo_loaded x_loaded ctx_head_loaded gates_loaded
            router_loaded rms_loaded w1_loaded w2_loaded
            ident_zero ident_ready causal_zero causal_slots causal_ready slots_zero moe_consts_ready
            ring_filled act_drained dve_drained vector_steps
            ln1_var_ready ln1_rstd_ready xn_ready tanh_ready
            scores_ready shifted_ready exp_ready probs_ready attn_done x1_ready
            squares_done guard_max_ready guard_rows_ready guard_ready
            ctx_stack_zero probs_stack_zero ctx_hi_ready ctx_lo_ready ctx_repeat_ready
            warm_ready table_loaded h_base_ready h_scale_ready g_h_scale_ready g_h_ready g_moment_steps
            g_hT_filled g_hT_hi_ready g_hT_ready ratio_square_ready
            ratio_ready h_ready hT_filled hT_ready hT_full_ready hT_hi_ready rms_filled rms_ready
            logits_filled logits_ready router_exp_ready
            w1_full_ready w1_hi_ready w1_scaled_ready hidden_filled hidden_ready
            expert_done acc_done last_tile_done next_to_last_added result_ready stored
            g_batch_ready g_ctxT_filled g_ctxT_ready g_A_ready
            g_key_filled g_key_ready g_score_filled g_max_ready g_exp_ready g_prob_ready
            g_probT_filled g_probT_ready g_mix_filled g_mix_ready g_out_filled g_vector_steps
            g_stored g_loaded g_x1_ready""".split()
        S = {n: sem(n) for n in names}
        S["wk_loaded"], S["wq_loaded"] = ([sem(f"{w}_loaded{n}") for n in range(2)]
                                          for w in ("wk", "wq"))
        ctx_loaded = [sem(f"ctx_loaded{b}") for b in range(B)]

        def bank_of(job):
            return RING_JOBS.index(job) % RING_BANKS

        def evacuated(job):
            if job in DVE_JOBS:
                return S["dve_drained"], DVE_JOBS.index(job) + 1
            return S["act_drained"], ACT_JOBS.index(job) + 1

        def wait_bank_free(pe, job):
            n = RING_JOBS.index(job)
            if n >= RING_BANKS:
                pe.wait_ge(*evacuated(RING_JOBS[n - RING_BANKS]))

        def wait_filled(eng, job):
            eng.wait_ge(S["ring_filled"], RING_JOBS.index(job) + 1)

        def bank(job, cols=BANK, rows=P):
            return ring[0:rows, bank_of(job), 0:cols]

        def evacuation(job):
            kind = job.rstrip("0123456789.")
            if kind in ("wkT", "wqT", "wvT"):
                dst = {"wkT": wkT, "wqT": wqT, "wvT": wvT}[kind]
                n = int(job[3:])
                return [dst[:, 4 * n:4 * n + 4, :]], bank(job).rearrange("p (c d) -> p c d", c=4)
            if kind == "ctxT":
                return [ctx_headT_hi[:, :], ctx_headT_lo[:, :]], bank(job, B * Q)
            if kind == "xnT":
                return [xnT[:, :, 0:Q]], bank(job, TOKENS).rearrange("p (b q) -> p b q", b=B)
            if kind in "AM":
                g = int(job[1:])
                return ([dst[:, 4 * g:4 * g + 4, :] for dst in {"A": (A_hi, A_lo), "M": (M,)}[kind]],
                        bank(job).rearrange("p (c d) -> p c d", c=4))
            if kind == "K":
                return [keyproj[:, int(job[1:]), :]], bank(job, B * Q)
            if kind == "P":
                g = int(job.split(".")[1])
                src = bank(job, rows=Q).rearrange("p (h b s) -> p h b s", h=4, b=2)[:, :, :, 0:Q]
                return [probs_stack[row:row + Q, 4 * g:4 * g + 4, :]
                        .rearrange("p h (b q) -> p h b q", b=2) for row in (0, SLOT)], src
            bb, half = int(job.split(".")[1]), int(job.split(".")[2])
            return ([mixT[:, 8 * half:8 * half + 8, bb * Q:bb * Q + Q]],
                    bank(job, 8 * Q).rearrange("p (h q) -> p h q", h=8))

        block = ctx.enter_context(nc.Block())

        @block.sync
        def _(sp):
            for dst, name, loaded in ((wk, "L0_xattn_w_k", "wk_loaded"),
                                      (wq, "L0_xattn_w_q", "wq_loaded")):
                for n in range(2):
                    cols = slice(n * INNER // 2, (n + 1) * INNER // 2)
                    sp.dma_start(dst[:, cols], A[name][:, cols]).then_inc(S[loaded][n], 16)
            sp.dma_start(ctx_head[:, :, :],
                         A["ctx_1024"][:, 0:Q, :].rearrange("b k d -> k b d"))\
                .then_inc(S["ctx_head_loaded"], 16)
            sp.dma_start(x_rows[:, :, :],
                         A["x"].rearrange("b q d -> (b q) d").rearrange("(t p) d -> p t d", p=ROWS))\
                .then_inc(S["x_loaded"], 16)
            sp.dma_start(wo[:, :, :], A["L0_xattn_w_o"].rearrange("(c p) n -> p c n", p=P))\
                .then_inc(S["wo_loaded"], 16)
            sp.wait_ge(S["ring_filled"], RING_JOBS.index("wkT1") + 1)
            sp.dma_start(wv[:, :], A["L0_xattn_w_v"]).then_inc(S["wv_loaded"], 16)
            sp.dma_start(gate_col[:, 0:1], A["g_xattn"].partition_broadcast(P))\
                .then_inc(S["gates_loaded"], 16)
            sp.dma_start(gate_col[:, 1:2], A["g_ffn"].partition_broadcast(P))\
                .then_inc(S["gates_loaded"], 16)
            sp.dma_start(rms_rows[0:SHARED, :], A["L0_ffn_rms_w_s"]).then_inc(S["rms_loaded"], 16)
            sp.dma_start(rms_rows[SHARED:EXPERTS, :], A["L0_ffn_rms_w"])\
                .then_inc(S["rms_loaded"], 16)
            sp.dma_start(router_w[:, :], A["L0_ffn_router_w"]).then_inc(S["router_loaded"], 16)
            for b in range(B):
                sp.dma_start(ctx_all[:, b, :],
                             A["ctx_1024"][b, :, :].rearrange("(p c) d -> p (c d)", c=KC))\
                    .then_inc(ctx_loaded[b], 16)
            sp.dma_start(w1[:, 0:SHARED, :], A["L0_ffn_w1_s"].rearrange("e p f -> p e f"))\
                .then_inc(S["w1_loaded"], 16)
            sp.dma_start(w2[:, 0:SHARED, :, :],
                         A["L0_ffn_w2_s"].rearrange("e (c p) n -> p e c n", p=P))\
                .then_inc(S["w2_loaded"], 16)
            sp.dma_start(w1[:, SHARED:EXPERTS, :], A["L0_ffn_w1"].rearrange("e p f -> p e f"))\
                .then_inc(S["w1_loaded"], 16)
            sp.dma_start(w2[:, SHARED:EXPERTS, :, :],
                         A["L0_ffn_w2"].rearrange("e (c p) n -> p e c n", p=P))\
                .then_inc(S["w2_loaded"], 16)
            out_rows = out.rearrange("b q d -> (b q) d").rearrange("(t p) d -> p t d", p=ROWS)
            for t in range(PAIRS):
                sp.wait_ge(S["result_ready"], t + 1)
                sp.dma_start(out_rows[:, t, :], moe[:, t, :]).then_inc(S["stored"], 16)
            sp.wait_ge(S["stored"], 16 * PAIRS)

        @block.gpsimd
        def _(pool):
            nc.gpsimd.memset(ident[:, :], 0.0).then_inc(S["ident_zero"], 1)
            nc.gpsimd.memset(minus_half[:, :], -0.5)
            pool.wait_ge(S["ident_zero"], 1)
            nc.gpsimd.affine_select(out=ident[:, :], in_=ident[:, :], compare_op=ALU.not_equal,
                                    fill=1.0, base=0, pattern=[[-1, P]], channel_multiplier=1)\
                .then_inc(S["ident_ready"], 1)
            nc.gpsimd.memset(xnT[:, :, :], 0.0).then_inc(S["slots_zero"], 1)
            nc.gpsimd.memset(mask_full[:, :], 0.0)
            nc.gpsimd.memset(causal_all[:, :, :], 0.0)
            nc.gpsimd.memset(guard_parts[:, :], 0.0).then_inc(S["causal_zero"], 1)
            pool.wait_ge(S["causal_zero"], 1)
            pool.wait_ge(S["ln1_var_ready"], 1)
            nc.gpsimd.tensor_tensor(ln_rstd[:, :], ln_var[:, :], minus_half[:, :], ALU.pow)\
                .then_inc(S["ln1_rstd_ready"], 1)
            pool.wait_ge(S["ln1_rstd_ready"], 1)
            for s in range(2):
                rows = mask_full[s * SLOT:(s + 1) * SLOT, :]
                nc.gpsimd.affine_select(out=rows, in_=rows, compare_op=ALU.is_ge, fill=MASKED / SCALE,
                                        base=0, pattern=[[-1, Q]], channel_multiplier=1)\
                    .then_inc(S["causal_slots"], 1)
                pool.wait_ge(S["causal_slots"], s + 1)
            nc.gpsimd.affine_select(out=causal_all[:, :, :], in_=causal_all[:, :, :],
                                    compare_op=ALU.is_ge, fill=MASKED, base=0,
                                    pattern=[[-1, KC], [-KC, 5]], channel_multiplier=1)
            nc.gpsimd.tensor_copy(mask[:, :], mask_full[:, :])
            nc.gpsimd.tensor_copy(ident_r[:, :], ident[:, :]).then_inc(S["causal_ready"], 1)
            nc.gpsimd.iota(rank[:, :, :], pattern=[[0, PAIRS], [-1, ROUTED]], base=ROUTED,
                           channel_multiplier=0, allow_small_or_imprecise_dtypes=True)
            nc.gpsimd.memset(plus_half[:, :], 0.5).then_inc(S["moe_consts_ready"], 1)

            def scale_w1(slot, e, weights, factors):
                scale = factors.to_broadcast([P, HIDDEN])
                nc.gpsimd.tensor_tensor(w1_full[:, :], weights, scale, ALU.mult)\
                    .then_inc(S["w1_full_ready"], 1)
                nc.gpsimd.tensor_tensor(w1_hi[slot][:, :], weights, scale, ALU.mult)\
                    .then_inc(S["w1_hi_ready"], 1)
                pool.wait_ge(S["w1_hi_ready"], e + 1)
                pool.wait_ge(S["w1_full_ready"], e + 1)
                nc.gpsimd.tensor_tensor(w1_lo[slot][:, :], w1_full[:, :],
                                        w1_hi[slot][:, :].bitcast(FP32), ALU.subtract)\
                    .then_inc(S["w1_scaled_ready"], 1)

            def scale_w1_static(e):
                if e:
                    pool.wait_ge(S["w1_scaled_ready"], e)
                scale_w1(e % 2, e, w1[:, e, :], rms_cols[:, e:e + 1])

            nc.gpsimd.memset(ctx_stack[:, :, :].bitcast(FP32), 0.0).then_inc(S["ctx_stack_zero"], 1)
            nc.gpsimd.memset(probs_stack[:, :, :].bitcast(FP32), 0.0)\
                .then_inc(S["probs_stack_zero"], 1)
            pool.wait_ge(S["ctx_stack_zero"], 1)
            pool.wait_ge(S["ctx_head_loaded"], 16)
            nc.gpsimd.tensor_copy(ctx_stack[0:Q, :, :], ctx_head[:, :, :])\
                .then_inc(S["ctx_hi_ready"], 1)
            pool.wait_ge(S["ctx_hi_ready"], 1)
            nc.gpsimd.tensor_tensor(ctx_lo[:, :, :], ctx_head[:, :, :],
                                    ctx_stack[0:Q, :, :].bitcast(FP32), ALU.subtract)\
                .then_inc(S["ctx_lo_ready"], 1)

            pool.wait_ge(S["rms_ready"], 1)
            pool.wait_ge(S["w1_loaded"], 32)
            for e in range(2):
                scale_w1_static(e)
            pool.wait_ge(S["moe_consts_ready"], 1)
            for t in range(PAIRS):
                pool.wait_ge(S["h_base_ready"], t + 1)
                nc.gpsimd.tensor_tensor(h_scale[:, t:t + 1], h_base[:, t:t + 1],
                                        minus_half[:, 0:1], ALU.pow)\
                    .then_inc(S["h_scale_ready"], 1)
            nc.gpsimd.tensor_tensor(h_scale[:, 0:PAIRS - 1], h_base[:, 0:PAIRS - 1],
                                    minus_half[:, 0:PAIRS - 1], ALU.pow)\
                .then_inc(S["g_h_scale_ready"], 1)
            pool.wait_ge(S["ratio_square_ready"], 1)
            nc.gpsimd.tensor_tensor(ratio[:, :], ratio_square[:, :], plus_half[:, :], ALU.pow)\
                .then_inc(S["ratio_ready"], 1)
            pool.wait_ge(S["hidden_filled"], 1)
            scale_w1_static(2)
            with pool.Fori(0, LOOP_STEPS) as i:
                for u in range(4):
                    e = i * 4 + (LOOP_FROM + u)
                    pool.wait_ge(S["hidden_filled"], e - 1)
                    pool.wait_ge(S["w1_scaled_ready"], e)
                    scale_w1((LOOP_FROM + u) % 2, e,
                             w1[:, bass.ds(e, 1), :].rearrange("p a f -> p (a f)"),
                             rms_cols[:, bass.ds(e, 1)])
            pool.wait_ge(S["hidden_filled"], EXPERTS - 2)
            scale_w1_static(EXPERTS - 1)

        @block.tensor
        def _(pe):
            pe.wait_ge(S["warm_ready"], 1)
            def keep_warm(products, dst):
                for _n in range(products):
                    nc.tensor.matmul(dst, warm[:, :], warm[:, :], start=True, stop=True)

            keep_warm(WARM_PRODUCTS, misc_ps[:, 0:P])
            pe.wait_ge(S["ident_ready"], 1)

            def transpose_weights(name, src, n):
                job = f"{name}{n}"
                wait_bank_free(pe, job)
                for i in range(4):
                    c = 4 * n + i
                    last = nc.tensor.transpose(ring[:, bank_of(job), i * P:(i + 1) * P],
                                               src[:, c * P:(c + 1) * P], ident[:, :])
                last.then_inc(S["ring_filled"], 1)

            for n in range(2):
                pe.wait_ge(S["wk_loaded"][n], 16)
                transpose_weights("wkT", wk, n)
            for n in range(2):
                pe.wait_ge(S["wq_loaded"][n], 16)
                transpose_weights("wqT", wq, n)

            pe.wait_ge(S["ctx_head_loaded"], 16)
            wait_bank_free(pe, "ctxT")
            for b in range(B):
                last = nc.tensor.transpose(ring[:, bank_of("ctxT"), b * Q:(b + 1) * Q],
                                           ctx_head[:, b, :], ident[0:Q, 0:Q])
            last.then_inc(S["ring_filled"], 1)

            for g in range(GROUPS):
                if g % 2 == 0:
                    pe.wait_ge(*evacuated(f"wkT{g // 2}"))
                    pe.wait_ge(*evacuated(f"wqT{g // 2}"))
                wait_bank_free(pe, f"A{g}")
                r = HEAD * (g % 2)
                for i in range(4):
                    c = head_of(g, i) // 2
                    last = nc.tensor.matmul(ring[:, bank_of(f"A{g}"), i * D:(i + 1) * D],
                                            wkT[r:r + HEAD, c, :], wqT[r:r + HEAD, c, :],
                                            start=True, stop=True)
                last.then_inc(S["ring_filled"], 1)

            def project_keys(s):
                job = f"K{s}"
                if s % 4 == 0:
                    pe.wait_ge(*evacuated(f"A{s // 4}"))
                if s == 0:
                    pe.wait_ge(*evacuated("ctxT"))
                wait_bank_free(pe, job)
                sums = ring[:, bank_of(job), 0:B * Q]
                nc.tensor.matmul(sums, A_hi[:, s, :], ctx_headT_hi[:, :], start=True, stop=False)
                nc.tensor.matmul(sums, A_hi[:, s, :], ctx_headT_lo[:, :], start=False, stop=False)
                nc.tensor.matmul(sums, A_lo[:, s, :], ctx_headT_hi[:, :], start=False, stop=True)\
                    .then_inc(S["ring_filled"], 1)

            for s in range(6):
                project_keys(s)
            pe.wait_ge(S["xn_ready"], 1)
            wait_bank_free(pe, "xnT")
            for t in range(PAIRS):
                last = nc.tensor.transpose(ring[:, bank_of("xnT"), t * ROWS:(t + 1) * ROWS],
                                           xn_rows[:, t, :], ident[0:ROWS, 0:ROWS])
            last.then_inc(S["ring_filled"], 1)
            def scores(t, half):
                if t:
                    pe.wait_ge(S["shifted_ready"], 2 * (t - 1) + half + 1)
                nc.tensor.matmul(score_ps[:, half, 0:8 * Q], ident_r[:, :],
                                 mask[:, :].unsqueeze(1).to_broadcast([P, 8, Q]),
                                 start=True, stop=False)
                for bb in range(2):
                    b = 2 * t + bb
                    last = nc.tensor.matmul(
                        score_ps[bb * SLOT:(bb + 1) * SLOT, half, 0:8 * Q],
                        xnT[:, b, :], keyproj[:, 8 * half:8 * half + 8, b * Q:(b + 1) * Q],
                        start=False, stop=True)
                last.then_inc(S["scores_ready"], 1)

            for s in range(6, 10):
                project_keys(s)
            pe.wait_ge(*evacuated("xnT"))
            pe.wait_ge(S["causal_ready"], 1)
            for s in (6, 7):
                pe.wait_ge(*evacuated(f"K{s}"))
            scores(0, 0)
            for s in range(10, HEADS):
                project_keys(s)
            pe.wait_ge(S["wv_loaded"], 16)
            for n in range(2):
                transpose_weights("wvT", wv, n)
            for s in (14, 15):
                pe.wait_ge(*evacuated(f"K{s}"))
            scores(0, 1)

            def transpose_probs(t):
                for g in range(GROUPS):
                    pe.wait_ge(S["probs_ready"], 2 * t + g // 2 + 1)
                    job = f"P{t}.{g}"
                    wait_bank_free(pe, job)
                    for i in range(4):
                        last = nc.tensor.transpose(ring[0:Q, bank_of(job), i * P:(i + 1) * P],
                                                   probs[:, t % 2, 4 * g + i, :], ident[:, :])
                    last.then_inc(S["ring_filled"], 1)

            def mix_context(t, half):
                pe.wait_ge(*evacuated(f"P{t}.{2 * half}"))
                pe.wait_ge(*evacuated(f"P{t}.{2 * half + 1}"))
                for bb in range(2):
                    job = f"C{t}.{bb}.{half}"
                    wait_bank_free(pe, job)
                    sums = ring[:, bank_of(job), 0:8 * Q]
                    heads, cols = slice(8 * half, 8 * half + 8), slice(bb * Q, (bb + 1) * Q)
                    nc.tensor.matmul(sums, ctx_stack[:, 2 * t + bb, :],
                                     probs_stack[:, heads, cols], start=True, stop=False)
                    nc.tensor.matmul(sums, ctx_lo[:, 2 * t + bb, :],
                                     probs_stack[0:Q, heads, cols], start=False, stop=True)\
                        .then_inc(S["ring_filled"], 1)

            def attention_out(t):
                if t == 0:
                    pe.wait_ge(*evacuated("M3"))
                    pe.wait_ge(*evacuated("M2"))
                else:
                    pe.wait_ge(S["x1_ready"], t)
                for s in range(HEADS):
                    if s % 8 == 0:
                        for bb in range(2):
                            pe.wait_ge(*evacuated(f"C{t}.{bb}.{s // 8}"))
                    last = nc.tensor.matmul(attn_ps[0:ROWS, 0:D], mixT[:, s, :], M[:, s, :],
                                            start=(s == 0), stop=(s == HEADS - 1))
                last.then_inc(S["attn_done"], 1)

            def transpose_rows(part, filled):
                tiles, cols, sums = h_parts[part]
                for t in tiles:
                    last = nc.tensor.transpose(sums[:, t * ROWS:(t + 1) * ROWS], h_rows[:, t, :],
                                               ident[0:ROWS, 0:ROWS])
                last.then_inc(filled, 1)

            pe.wait_ge(S["wo_loaded"], 16)
            for g in range(GROUPS):
                if g % 2 == 0:
                    pe.wait_ge(*evacuated(f"wvT{g // 2}"))
                wait_bank_free(pe, f"M{g}")
                r = HEAD * (g % 2)
                for i in range(4):
                    c = head_of(g, i) // 2
                    last = nc.tensor.matmul(ring[:, bank_of(f"M{g}"), i * D:(i + 1) * D],
                                            wvT[r:r + HEAD, c, :], wo[r:r + HEAD, c, :],
                                            start=True, stop=True)
                last.then_inc(S["ring_filled"], 1)
            pe.wait_ge(S["rms_loaded"], 32)
            nc.tensor.transpose(misc_ps[:, 0:EXPERTS], rms_rows[:, :], ident[0:EXPERTS, 0:EXPERTS])\
                .then_inc(S["rms_filled"], 1)
            for t in range(PAIRS):
                transpose_probs(t)
                if t == PAIRS - 1:
                    pe.wait_ge(S["guard_max_ready"], 1)
                    pe.wait_ge(S["rms_ready"], 1)
                    for k in range(2):
                        last = nc.tensor.transpose(misc_ps[0:1, k * P:(k + 1) * P],
                                                   guard_max[:, k:k + 1], ident[:, :])
                    last.then_inc(S["guard_rows_ready"], 1)
                    pe.wait_ge(S["shifted_ready"], 2 * PAIRS)
                    keep_warm(SPLIT_PRODUCTS, score_ps[:, 0, 0:P])
                if t == 0:
                    pe.wait_ge(S["ctx_lo_ready"], 1)
                    pe.wait_ge(S["ctx_repeat_ready"], 1)
                for half in range(2):
                    if t + 1 < PAIRS:
                        scores(t + 1, half)
                    mix_context(t, half)
                if t == PAIRS - 1:
                    pe.wait_ge(S["guard_ready"], 1)
                    ok = pe.value_load(guard_ok[0:1, 0:1], min_val=0, max_val=1)
                    pe.wait_ge(S["h_ready"], PAIRS - 1)
                    transpose_rows(0, S["hT_filled"])
                attention_out(t)

            with pe.If(ok < 1):
                with pe.Fori(0, B) as b:
                    pe.wait_ge(S["g_batch_ready"], b + 1)
                    for c in range(KC):
                        last = nc.tensor.transpose(ring[:, c // 4, (c % 4) * KP:(c % 4 + 1) * KP],
                                                   g_ctx[:, c, :], ident[0:KP, 0:KP])
                    last.then_inc(S["g_ctxT_filled"], 1)
                    with pe.Fori(0, HEADS) as h:
                        n = b * HEADS + h
                        pe.wait_ge(S["g_ctxT_ready"], b + 1)
                        pe.wait_ge(S["g_A_ready"], n + 1)
                        for k in range(3):
                            last = nc.tensor.matmul(ring[:, k, 0:4 * KP], g_AT[:, :],
                                                    g_ctxT[:, k * 4 * KP:(k + 1) * 4 * KP],
                                                    start=True, stop=True)
                        last.then_inc(S["g_key_filled"], 1)
                        pe.wait_ge(S["g_key_ready"], n + 1)
                        for k in range(3):
                            last = nc.tensor.matmul(ring[0:Q, k, 0:4 * KP], g_xnT[:, :],
                                                    g_key[:, k * 4 * KP:(k + 1) * 4 * KP],
                                                    start=True, stop=True)
                        last.then_inc(S["g_score_filled"], 1)
                        pe.wait_ge(S["g_prob_ready"], n + 1)
                        for c in range(KC):
                            last = nc.tensor.matmul(
                                score_ps[0:KP, c // 8, (c % 8) * Q:(c % 8 + 1) * Q],
                                g_prob[:, c * KP:(c + 1) * KP], ident[0:Q, 0:Q],
                                start=True, stop=True)
                        last.then_inc(S["g_probT_filled"], 1)
                        pe.wait_ge(S["g_probT_ready"], n + 1)
                        for c in range(KC):
                            last = nc.tensor.matmul(attn_ps[:, 0:Q], g_ctx[:, c, :], g_probT[:, c, :],
                                                    start=(c == 0), stop=(c == KC - 1))
                        last.then_inc(S["g_mix_filled"], 1)
                        pe.wait_ge(S["g_mix_ready"], n + 1)
                        nc.tensor.matmul(misc_ps[0:Q, 0:D], g_mixT[:, :],
                                         M[:, bass.ds(h, 1), :].rearrange("p a d -> p (a d)"),
                                         start=True, stop=True).then_inc(S["g_out_filled"], 1)
                pe.wait_ge(S["g_vector_steps"], B * G_BATCH_STEPS)

                pe.wait_ge(S["g_h_ready"], 1)
                transpose_rows(0, S["g_hT_filled"])
                pe.wait_ge(S["g_hT_ready"], 1)

            def router_logits(part):
                pe.wait_ge(S["hT_full_ready"], part + 1)
                for t in h_parts[part][0]:
                    last = nc.tensor.matmul(misc_ps[0:ROWS, logit_col(t):logit_col(t + 1)],
                                            hT[:, t * ROWS:(t + 1) * ROWS], router_w[:, :],
                                            start=True, stop=True)
                return last

            def hidden_products(slot, cols=slice(0, TOKENS)):
                for c in range(2):
                    hi, lo = (w[slot][:, c * P:(c + 1) * P] for w in (w1_hi, w1_lo))
                    sums = ring[:, 2 * slot + c, cols]
                    nc.tensor.matmul(sums, hi, hT_hi[:, cols], start=True, stop=False)
                    nc.tensor.matmul(sums, hi, hT_lo[:, cols], start=False, stop=False)
                    last = nc.tensor.matmul(sums, lo, hT_hi[:, cols], start=False, stop=True)
                return last

            def output_tile(dst, slot, t, w2_chunk):
                for c in range(2):
                    last = nc.tensor.matmul(dst, hidden[slot][:, c, t * ROWS:(t + 1) * ROWS],
                                            w2_chunk(c), start=(c == 0), stop=(c == 1))
                return last

            def expert_output(slot, w2_chunk):
                for t in range(PAIRS):
                    last = output_tile(score_ps[0:ROWS, slot, t * D:(t + 1) * D], slot, t, w2_chunk)
                last.then_inc(S["expert_done"], 1)

            def static_w2(e):
                return lambda c: w2[:, e, c, :]

            pe.wait_ge(S["hT_ready"], 1)
            for e in range(2):
                pe.wait_ge(S["w1_scaled_ready"], e + 1)
                hidden_products(e, h_parts[0][1])
            pe.wait_ge(S["router_loaded"], 16)
            router_logits(0)
            pe.wait_ge(S["x1_ready"], PAIRS)
            pe.wait_ge(S["h_ready"], PAIRS)
            transpose_rows(1, S["hT_filled"])
            keep_warm(SPLIT_PRODUCTS, score_ps[:, 0, 0:P])
            pe.wait_ge(S["hT_ready"], 2)
            hidden_products(0, h_parts[1][1]).then_inc(S["hidden_filled"], 1)
            router_logits(1).then_inc(S["logits_filled"], 1)
            hidden_products(1, h_parts[1][1]).then_inc(S["hidden_filled"], 1)
            pe.wait_ge(S["w2_loaded"], 32)
            pe.wait_ge(S["hidden_ready"], 1)
            expert_output(0, static_w2(0))
            pe.wait_ge(S["w1_scaled_ready"], 3)
            hidden_products(0).then_inc(S["hidden_filled"], 1)
            pe.wait_ge(S["hidden_ready"], 2)
            expert_output(1, static_w2(1))
            with pe.Fori(0, LOOP_STEPS) as i:
                for u in range(4):
                    e = i * 4 + (LOOP_FROM + u)
                    slot = (LOOP_FROM + u) % 2
                    pe.wait_ge(S["w1_scaled_ready"], e + 1)
                    pe.wait_ge(S["hidden_ready"], e - 1)
                    hidden_products(slot).then_inc(S["hidden_filled"], 1)
                    pe.wait_ge(S["hidden_ready"], e)
                    pe.wait_ge(S["acc_done"], e - 2)
                    expert_output(1 - slot, lambda c: w2[:, bass.ds(e - 1, 1), c, :]
                                  .rearrange("p a n -> p (a n)"))
            pe.wait_ge(S["w1_scaled_ready"], EXPERTS)
            pe.wait_ge(S["hidden_ready"], EXPERTS - 2)
            hidden_products((EXPERTS - 1) % 2).then_inc(S["hidden_filled"], 1)
            for k in range(2):
                e = EXPERTS - 2 + k
                pe.wait_ge(S["hidden_ready"], e + 1)
                pe.wait_ge(S["acc_done"], e - 1)
                for t in range(PAIRS):
                    output_tile(last_tiles[k * PAIRS + t], e % 2, t, static_w2(e))\
                        .then_inc(S["last_tile_done"], 1)

        @block.scalar
        def _(act):
            act.wait_ge(S["warm_ready"], 1)
            nc.scalar.activation(table_probe[:, :], warm[0:1, 0:1], ACT.Exp)\
                .then_inc(S["table_loaded"], 1)

            def evacuate_own(jobs):
                for job in jobs:
                    if job in ACT_JOBS:
                        dst, src = evacuation(job)
                        wait_filled(act, job)
                        nc.scalar.activation(dst[0], src, ACT.Copy).then_inc(S["act_drained"], 1)

            def square_sum(n, column, src):
                if n:
                    act.wait_ge(S["squares_done"], n)
                rows, cols = src.shape[0], src.shape[1]
                nc.scalar.activation(square_junk[0:rows, 0:cols], src, ACT.Square,
                                     accum_out=guard_parts[0:rows, column:column + 1])\
                    .then_inc(S["squares_done"], 1)

            def context_squares(batches):
                for b in batches:
                    act.wait_ge(ctx_loaded[b], 16)
                    square_sum(GROUPS + b, GROUPS + b, ctx_all[:, b, :])

            def softmax_exp(t, half):
                p = probs[:, t % 2, 8 * half:8 * half + 8, :]
                act.wait_ge(S["shifted_ready"], 2 * t + half + 1)
                nc.scalar.activation(p, p, ACT.Exp, scale=SCALE).then_inc(S["exp_ready"], 1)

            evacuate_own(RING_JOBS[:RING_JOBS.index("K2")])
            act.wait_ge(S["causal_zero"], 1)
            for g in range(GROUPS):
                evacuate_own([f"K{2 * g + 2}"])
                act.wait_ge(*evacuated(f"A{g}"))
                square_sum(g, g, A_hi[:, 4 * g:4 * g + 4, :].rearrange("p h d -> p (h d)")
                           .bitcast(FP32))
            evacuate_own(["K10"])
            act.wait_ge(S["ctx_stack_zero"], 1)
            nc.scalar.activation(ctx_stack[SLOT:STACK, :, :], ctx_head[:, :, :], ACT.Copy)\
                .then_inc(S["ctx_repeat_ready"], 1)
            evacuate_own(["K12"])
            softmax_exp(0, 0)
            evacuate_own(["K14"])
            context_squares([0])
            evacuate_own(["wvT0", "wvT1"])
            softmax_exp(0, 1)
            evacuate_own(["M0", "M2"])
            act.wait_ge(S["gates_loaded"], 32)
            act.wait_ge(S["table_loaded"], 1)
            nc.scalar.activation(tanh_col[:, :], gate_col[:, :], ACT.Tanh).then_inc(S["tanh_ready"], 1)
            context_squares([1])
            act.wait_ge(S["probs_stack_zero"], 1)
            for t in range(PAIRS):
                evacuate_own([f"P{t}.{g}" for g in range(GROUPS)])
                context_squares([[2], [4], [6], []][t])
                evacuate_own([f"C{t}.0.0", f"C{t}.1.0", f"C{t}.0.1"])
                if t + 1 < PAIRS:
                    softmax_exp(t + 1, 0)
                evacuate_own([f"C{t}.1.1"])
                if t + 1 < PAIRS:
                    softmax_exp(t + 1, 1)
                context_squares([[3], [5], [7], []][t])

            def round_rows(part, filled, ready):
                _tiles, cols, sums = h_parts[part]
                act.wait_ge(filled, part + 1)
                nc.scalar.activation(hT_hi[:, cols], sums[:, cols], ACT.Copy).then_inc(ready, 1)

            round_rows(0, S["hT_filled"], S["hT_hi_ready"])

            act.wait_ge(S["guard_ready"], 1)
            ok = act.value_load(guard_ok[0:1, 0:1], min_val=0, max_val=1)
            with act.If(ok < 1):
                with act.Fori(0, B) as b:
                    act.wait_ge(S["g_ctxT_filled"], b + 1)
                    nc.scalar.activation(g_ctxT.rearrange("p (k n) -> p k n", k=3),
                                         ring[:, 0:3, 0:4 * KP], ACT.Copy)\
                        .then_inc(S["g_ctxT_ready"], 1)
                    with act.Fori(0, HEADS) as h:
                        n = b * HEADS + h
                        act.wait_ge(S["g_key_filled"], n + 1)
                        nc.scalar.activation(g_key.rearrange("p (k n) -> p k n", k=3),
                                             ring[:, 0:3, 0:4 * KP], ACT.Copy)\
                            .then_inc(S["g_key_ready"], 1)
                        act.wait_ge(S["g_max_ready"], n + 1)
                        nc.scalar.activation(g_prob, g_prob, ACT.Exp, bias=g_max[:, 0:1],
                                             accum_out=g_sum[:, 0:1]).then_inc(S["g_exp_ready"], 1)
                        act.wait_ge(S["g_probT_filled"], n + 1)
                        nc.scalar.activation(g_probT[:, 0:8, :].rearrange("p c q -> p (c q)"),
                                             score_ps[0:KP, 0, 0:8 * Q], ACT.Copy)
                        nc.scalar.activation(g_probT[:, 8:KC, :].rearrange("p c q -> p (c q)"),
                                             score_ps[0:KP, 1, 0:(KC - 8) * Q], ACT.Copy)\
                            .then_inc(S["g_probT_ready"], 1)
                        act.wait_ge(S["g_mix_filled"], n + 1)
                        nc.scalar.activation(g_mixT[:, :], attn_ps[:, 0:Q], ACT.Copy)\
                            .then_inc(S["g_mix_ready"], 1)
                    act.wait_ge(S["g_vector_steps"], (b + 1) * G_BATCH_STEPS)
                    act.dma_start(g_attn_dram[bass.ds(b * Q, Q), :], g_acc[:, :])\
                        .then_inc(S["g_stored"], 16)
                act.wait_ge(S["g_stored"], 16 * B)
                act.dma_start(attn_all[:, :, :], g_attn_dram.rearrange("(t p) d -> p t d", p=ROWS))\
                    .then_inc(S["g_loaded"], 16)
                act.wait_ge(S["g_loaded"], 16)
                round_rows(0, S["g_hT_filled"], S["g_hT_hi_ready"])
                act.wait_ge(S["g_hT_ready"], 1)

            def copy_rows(part):
                _tiles, cols, sums = h_parts[part]
                act.wait_ge(S["hT_ready"], part + 1)
                nc.scalar.activation(hT[:, cols], sums[:, cols], ACT.Copy)\
                    .then_inc(S["hT_full_ready"], 1)

            act.wait_ge(S["table_loaded"], 1)
            nc.scalar.activation(table_probe[:, :], warm[0:1, 0:1], ACT.Silu)\
                .then_inc(S["table_loaded"], 1)
            act.wait_ge(S["x1_ready"], PAIRS)
            copy_rows(0)
            round_rows(1, S["hT_filled"], S["hT_hi_ready"])
            copy_rows(1)
            def silu(slot):
                nc.scalar.activation(hidden[slot], ring[:, 2 * slot:2 * slot + 2, 0:TOKENS],
                                     ACT.Silu).then_inc(S["hidden_ready"], 1)

            for e in range(LOOP_FROM):
                if e == 2:
                    act.wait_ge(S["logits_ready"], 1)
                    nc.scalar.activation(expo[:, :, :], shifted[:, :, :], ACT.Exp)\
                        .then_inc(S["router_exp_ready"], 1)
                act.wait_ge(S["hidden_filled"], e + 1)
                if e >= 2:
                    act.wait_ge(S["expert_done"], e - 1)
                silu(e % 2)
            with act.Fori(0, LOOP_STEPS) as i:
                for u in range(4):
                    e = i * 4 + (LOOP_FROM + u)
                    act.wait_ge(S["hidden_filled"], e + 1)
                    act.wait_ge(S["expert_done"], e - 1)
                    silu((LOOP_FROM + u) % 2)
            act.wait_ge(S["hidden_filled"], EXPERTS)
            act.wait_ge(S["expert_done"], EXPERTS - 2)
            silu((EXPERTS - 1) % 2)

        @block.vector
        def _(dve):
            steps = [0]

            def then_wait(instruction):
                steps[0] += 1
                instruction.then_inc(S["vector_steps"], 1)
                dve.wait_ge(S["vector_steps"], steps[0])

            def evacuate_own(jobs):
                for job in jobs:
                    if job in DVE_JOBS:
                        dst, src = evacuation(job)
                        if job in SPLIT_JOBS:
                            dve.wait_ge(S["act_drained"], ACT_JOBS.index(job) + 1)
                            nc.vector.tensor_tensor(dst[1], src, dst[0].bitcast(FP32), ALU.subtract)\
                                .then_inc(S["dve_drained"], 1)
                        else:
                            wait_filled(dve, job)
                            nc.vector.tensor_copy(dst[0], src).then_inc(S["dve_drained"], 1)

            def moments(rows):
                for t in range(PAIRS):
                    last = nc.vector.bn_stats(ln_stats[:, t, :], rows[:, t, :])
                then_wait(last)
                for t in range(PAIRS):
                    last = nc.vector.bn_aggr(ln_mv[:, t, :], ln_stats[:, t, :])
                then_wait(last)

            nc.vector.memset(warm[:, :], 0.0).then_inc(S["warm_ready"], 1)
            evacuate_own(["wkT1", "wqT1"])
            dve.wait_ge(S["x_loaded"], 16)
            moments(x_rows)
            nc.vector.tensor_scalar(ln_var[:, :], ln_mv[:, :, 1], LN_EPS, None, ALU.add)\
                .then_inc(S["ln1_var_ready"], 1)
            evacuate_own(["ctxT"] + [f"A{g}" for g in range(GROUPS)] + ["K1"])
            dve.wait_ge(S["ln1_rstd_ready"], 1)
            for t in range(PAIRS):
                last = nc.vector.tensor_scalar(xn_rows[:, t, :], x_rows[:, t, :], ln_mv[:, t, 0:1],
                                               ln_rstd[:, t:t + 1], ALU.subtract, ALU.mult)
            last.then_inc(S["xn_ready"], 1)
            dve.wait_ge(S["slots_zero"], 1)

            def half_heads(half):
                return slice(8 * half, 8 * half + 8)

            def per_head(column, half):
                return column[:, half_heads(half)].unsqueeze(2).to_broadcast([P, 8, Q])

            def softmax_shift(t, halves=(0, 1)):
                sums = [score_ps[:, half, 0:8 * Q].rearrange("p (h k) -> p h k", h=8)
                        for half in range(2)]
                for half in halves:
                    dve.wait_ge(S["scores_ready"], 2 * t + half + 1)
                    last = nc.vector.tensor_reduce(row_max[:, half_heads(half)], sums[half], AX.X,
                                                   ALU.max)
                then_wait(last)
                if t >= 2:
                    dve.wait_ge(S["ring_filled"], RING_JOBS.index(f"P{t - 2}.{GROUPS - 1}") + 1)
                for half in halves:
                    nc.vector.tensor_tensor(probs[:, t % 2, half_heads(half), :], sums[half],
                                            per_head(row_max, half), ALU.subtract)\
                        .then_inc(S["shifted_ready"], 1)

            def softmax_normalise(t, halves=(0, 1)):
                for half in halves:
                    dve.wait_ge(S["exp_ready"], 2 * t + half + 1)
                    last = nc.vector.tensor_reduce(row_sum[:, half_heads(half)],
                                                   probs[:, t % 2, half_heads(half), :], AX.X, ALU.add)
                then_wait(last)
                heads = slice(8 * halves[0], 8 * halves[-1] + 8)
                then_wait(nc.vector.reciprocal(row_inv[:, heads], row_sum[:, heads]))
                for half in halves:
                    p = probs[:, t % 2, half_heads(half), :]
                    nc.vector.tensor_tensor(p, p, per_head(row_inv, half), ALU.mult)\
                        .then_inc(S["probs_ready"], 1)

            def first_residual(t):
                dve.wait_ge(S["attn_done"], t + 1)
                nc.vector.scalar_tensor_tensor(out=x1[:, t, :], in0=attn_ps[0:ROWS, 0:D],
                                               scalar=tanh_col[0:ROWS, 0:1], in1=x_rows[:, t, :],
                                               op0=ALU.mult, op1=ALU.add)\
                    .then_inc(S["x1_ready"], 1)

            def second_moments(tiles, after_step=then_wait):
                for t in tiles:
                    last = nc.vector.bn_stats(ln_stats[:, t, :], x1[:, t, :])
                after_step(last)
                for t in tiles:
                    last = nc.vector.bn_aggr(ln_mv[:, t, :], ln_stats[:, t, :])
                after_step(last)
                cols = slice(tiles[0], tiles[-1] + 1)
                return nc.vector.tensor_scalar(h_base[:, cols], ln_mv[:, cols, 1],
                                               1.0 + RMS_EPS, LN_EPS * RMS_EPS, ALU.mult, ALU.add)

            def normalised(t):
                return nc.vector.tensor_scalar(h_rows[:, t, :], x1[:, t, :], ln_mv[:, t, 0:1],
                                               h_scale[:, t:t + 1], ALU.subtract, ALU.mult)

            def subtract_hi(part, hi_ready, ready):
                _tiles, cols, sums = h_parts[part]
                dve.wait_ge(hi_ready, part + 1)
                nc.vector.tensor_tensor(hT_lo[:, cols], sums[:, cols], hT_hi[:, cols].bitcast(FP32),
                                        ALU.subtract).then_inc(ready, 1)

            evacuate_own(RING_JOBS[RING_JOBS.index("K2"):RING_JOBS.index("K10")])
            softmax_shift(0, [0])
            evacuate_own(["K11", "K13", "K15"])
            softmax_normalise(0, [0])
            softmax_shift(0, [1])
            evacuate_own(["M1"])
            softmax_normalise(0, [1])
            evacuate_own(["M3"])
            dve.wait_ge(S["rms_filled"], 1)
            nc.vector.tensor_copy(rms_cols[:, :], misc_ps[:, 0:EXPERTS]).then_inc(S["rms_ready"], 1)
            dve.wait_ge(S["tanh_ready"], 1)
            nc.vector.tensor_copy(gates[:, 0:SHARED, :], tanh_col[0:ROWS, 1:2].unsqueeze(2)
                                  .to_broadcast([ROWS, SHARED, PAIRS]))
            for t in range(PAIRS):
                if t == PAIRS - 1:
                    dve.wait_ge(S["squares_done"], GROUPS + B)
                    nc.vector.tensor_reduce(guard_max[:, 0:1], guard_parts[:, 0:GROUPS], AX.X, ALU.max)
                    nc.vector.tensor_reduce(guard_max[:, 1:2], guard_parts[:, GROUPS:GROUPS + B],
                                            AX.X, ALU.max).then_inc(S["guard_max_ready"], 1)
                evacuate_own([f"P{t}.{g}" for g in range(GROUPS)])
                if t == PAIRS - 1:
                    dve.wait_ge(S["guard_rows_ready"], 1)
                    then_wait(nc.vector.tensor_reduce(
                        guard_pair[:, :], misc_ps[0:1, 0:2 * P].rearrange("p (k n) -> p k n", k=2),
                        AX.X, ALU.max))
                    then_wait(nc.vector.tensor_tensor(guard_prod[:, :], guard_pair[:, 0:1],
                                                      guard_pair[:, 1:2], ALU.mult))
                    nc.vector.tensor_scalar(guard_ok[:, :], guard_prod[:, :], GUARD_LIMIT, None,
                                            ALU.is_lt).then_inc(S["guard_ready"], 1)
                if t + 1 < PAIRS:
                    softmax_shift(t + 1)
                    softmax_normalise(t + 1)
                if t >= 1:
                    dve.wait_ge(S["h_scale_ready"], t)
                    normalised(t - 1).then_inc(S["h_ready"], 1)
                if t == PAIRS - 1:
                    dve.wait_ge(S["guard_ready"], 1)
                    ok = dve.value_load(guard_ok[0:1, 0:1], min_val=0, max_val=1)
                    subtract_hi(0, S["hT_hi_ready"], S["hT_ready"])
                first_residual(t)
                if t < PAIRS - 1:
                    dve.wait_ge(S["x1_ready"], t + 1)
                    second_moments([t]).then_inc(S["h_base_ready"], 1)

            with dve.If(ok < 1):
                with dve.Fori(0, B) as b:
                    nc.vector.memset(g_acc[:, :], 0.0).then_inc(S["g_vector_steps"], 1)
                    nc.vector.tensor_copy(g_xnT[:, :], xnT[:, bass.ds(b, 1), 0:Q]
                                          .rearrange("p a q -> p (a q)"))
                    nc.vector.tensor_copy(g_ctx.rearrange("p c d -> p (c d)"),
                                          ctx_all[:, bass.ds(b, 1), :].rearrange("p a n -> p (a n)"))\
                        .then_inc(S["g_batch_ready"], 1)
                    with dve.Fori(0, HEADS) as h:
                        n = b * HEADS + h
                        done = b * G_BATCH_STEPS + h * G_HEAD_STEPS + 1
                        nc.vector.tensor_tensor(
                            g_AT[:, :],
                            A_hi[:, bass.ds(h, 1), :].rearrange("p a d -> p (a d)").bitcast(FP32),
                            A_lo[:, bass.ds(h, 1), :].rearrange("p a d -> p (a d)").bitcast(FP32),
                            ALU.add).then_inc(S["g_A_ready"], 1)
                        dve.wait_ge(S["g_score_filled"], n + 1)
                        nc.vector.tensor_scalar(g_prob.rearrange("p (k n) -> p k n", k=3),
                                                ring[0:Q, 0:3, 0:4 * KP], SCALE, MASKED,
                                                ALU.mult, ALU.add).then_inc(S["g_vector_steps"], 1)
                        dve.wait_ge(S["g_vector_steps"], done + 1)
                        for k in range(3):
                            src = ring[0:Q, k, 0:4 * KP].rearrange("p (c n) -> p c n", c=4)
                            dst = g_prob[:, k * 4 * KP:(k + 1) * 4 * KP]
                            last = nc.vector.scalar_tensor_tensor(
                                out=dst.rearrange("p (c n) -> p c n", c=4)[:, :, 0:5],
                                in0=src[:, :, 0:5], scalar=SCALE,
                                in1=causal_all[:, 4 * k:4 * k + 4, :], op0=ALU.mult, op1=ALU.add)
                        last.then_inc(S["g_vector_steps"], 1)
                        dve.wait_ge(S["g_vector_steps"], done + 2)
                        nc.vector.tensor_reduce(g_max[:, :], g_prob, AX.X, ALU.max, negate=True)\
                            .then_inc(S["g_max_ready"], 1)
                        dve.wait_ge(S["g_exp_ready"], n + 1)
                        nc.vector.reciprocal(g_inv[:, :], g_sum[:, :])\
                            .then_inc(S["g_vector_steps"], 1)
                        dve.wait_ge(S["g_vector_steps"], done + 3)
                        nc.vector.tensor_scalar(g_prob, g_prob, g_inv[:, 0:1], None, ALU.mult)\
                            .then_inc(S["g_prob_ready"], 1)
                        dve.wait_ge(S["g_out_filled"], n + 1)
                        nc.vector.tensor_tensor(g_acc[:, :], g_acc[:, :], misc_ps[0:Q, 0:D], ALU.add)\
                            .then_inc(S["g_vector_steps"], 1)
                    dve.wait_ge(S["g_stored"], (b + 1) * 16)
                dve.wait_ge(S["g_loaded"], 16)
                for t in range(PAIRS):
                    last = nc.vector.scalar_tensor_tensor(
                        out=x1[:, t, :], in0=attn_all[:, t, :], scalar=tanh_col[0:ROWS, 0:1],
                        in1=x_rows[:, t, :], op0=ALU.mult, op1=ALU.add)
                last.then_inc(S["g_x1_ready"], 1)
                dve.wait_ge(S["g_x1_ready"], 1)
                g_steps = [0]

                def g_then_wait(instruction):
                    g_steps[0] += 1
                    instruction.then_inc(S["g_moment_steps"], 1)
                    dve.wait_ge(S["g_moment_steps"], g_steps[0])

                second_moments(range(PAIRS - 1), g_then_wait)

            dve.wait_ge(S["x1_ready"], PAIRS)
            second_moments([PAIRS - 1]).then_inc(S["h_base_ready"], 1)
            with dve.If(ok < 1):
                dve.wait_ge(S["g_h_scale_ready"], 1)
                for t in range(PAIRS - 1):
                    last = normalised(t)
                last.then_inc(S["g_h_ready"], 1)
                subtract_hi(0, S["g_hT_hi_ready"], S["g_hT_ready"])
            dve.wait_ge(S["h_scale_ready"], PAIRS)
            normalised(PAIRS - 1).then_inc(S["h_ready"], 1)

            then_wait(nc.vector.tensor_scalar(ln2_var[:, :], ln_mv[:, :, 1], LN_EPS, None, ALU.add))
            then_wait(nc.vector.reciprocal(ln2_inv[:, :], ln2_var[:, :]))
            nc.vector.tensor_tensor(ratio_square[:, :], h_base[:, :], ln2_inv[:, :], ALU.mult)\
                .then_inc(S["ratio_square_ready"], 1)
            subtract_hi(1, S["hT_hi_ready"], S["hT_ready"])

            def wide(col):
                return col[:, :].unsqueeze(2).to_broadcast([ROWS, PAIRS, ROUTED])

            def add_expert(slot, gate, before=moe):
                for t in range(PAIRS):
                    last = nc.vector.scalar_tensor_tensor(
                        out=moe[:, t, :], in0=score_ps[0:ROWS, slot, t * D:(t + 1) * D],
                        scalar=gate(t), in1=before[:, t, :], op0=ALU.mult, op1=ALU.add)
                last.then_inc(S["acc_done"], 1)

            def static_gate(e):
                return lambda t: gates[:, e, t:t + 1]

            dve.wait_ge(S["logits_filled"], 1)
            dve.wait_ge(S["ratio_ready"], 1)
            then_wait(nc.vector.tensor_tensor(
                logits[:, :, :],
                misc_ps[0:ROWS, logit_col(0):logit_col(PAIRS)].rearrange("p (t e) -> p t e", t=PAIRS),
                wide(ratio), ALU.mult))
            then_wait(nc.vector.tensor_reduce(logit_max[:, :], logits[:, :, :], AX.X, ALU.max))
            nc.vector.tensor_tensor(shifted[:, :, :], logits[:, :, :], wide(logit_max), ALU.subtract)\
                .then_inc(S["logits_ready"], 1)
            dve.wait_ge(S["expert_done"], 1)
            add_expert(0, static_gate(0), before=x1)
            dve.wait_ge(S["router_exp_ready"], 1)
            dve.wait_ge(S["moe_consts_ready"], 1)
            nc.vector.tensor_reduce(exp_sum[:, :], expo[:, :, :], AX.X, ALU.add)
            for i, values in enumerate((expo, rest)):
                then_wait(nc.vector.tensor_reduce(top[i][:, :], values[:, :, :], AX.X, ALU.max))
                then_wait(nc.vector.tensor_tensor(hit[i][:, :, :], values[:, :, :], wide(top[i]),
                                                  ALU.is_ge))
                then_wait(nc.vector.tensor_tensor(tie[i][:, :, :], hit[i][:, :, :], rank[:, :, :],
                                                  ALU.mult))
                then_wait(nc.vector.tensor_reduce(best_rank[i][:, :], tie[i][:, :, :], AX.X, ALU.max))
                then_wait(nc.vector.tensor_tensor(pick[i][:, :, :], tie[i][:, :, :],
                                                  wide(best_rank[i]), ALU.is_equal))
                if i == 0:
                    then_wait(nc.vector.scalar_tensor_tensor(
                        out=rest[:, :, :], in0=pick[0][:, :, :], scalar=-2.0, in1=expo[:, :, :],
                        op0=ALU.mult, op1=ALU.add))
            then_wait(nc.vector.tensor_tensor(pick[0][:, :, :], pick[0][:, :, :], pick[1][:, :, :],
                                              ALU.add))
            then_wait(nc.vector.tensor_tensor(chosen[:, :, :], pick[0][:, :, :], expo[:, :, :],
                                              ALU.mult))
            then_wait(nc.vector.tensor_reduce(top_sum[:, :], chosen[:, :, :], AX.X, ALU.add))
            then_wait(nc.vector.scalar_tensor_tensor(out=gate_den[:, :], in0=exp_sum[:, :],
                                                     scalar=GATE_EPS, in1=top_sum[:, :],
                                                     op0=ALU.mult, op1=ALU.add))
            then_wait(nc.vector.reciprocal(gate_inv[:, :], gate_den[:, :]))
            then_wait(nc.vector.tensor_scalar(gate_inv[:, :], gate_inv[:, :],
                                              tanh_col[0:ROWS, 1:2], None, ALU.mult))
            then_wait(nc.vector.tensor_tensor(
                gates[:, SHARED:EXPERTS, :].rearrange("p e t -> p t e"), chosen[:, :, :],
                wide(gate_inv), ALU.mult))

            dve.wait_ge(S["expert_done"], 2)
            dve.wait_ge(S["acc_done"], 1)
            add_expert(1, static_gate(1))
            with dve.Fori(0, LOOP_STEPS) as i:
                for u in range(4):
                    e = i * 4 + (2 + u)
                    dve.wait_ge(S["expert_done"], e + 1)
                    dve.wait_ge(S["acc_done"], e)
                    add_expert(u % 2, lambda t: gates[:, bass.ds(e, 1), t]
                               .rearrange("p a -> p a"))
            dve.wait_ge(S["acc_done"], EXPERTS - 2)
            for k in range(2):
                e = EXPERTS - 2 + k
                for t in range(PAIRS):
                    dve.wait_ge(S["last_tile_done"], k * PAIRS + t + 1)
                    if k == 1:
                        dve.wait_ge(S["next_to_last_added"], t + 1)
                    nc.vector.scalar_tensor_tensor(
                        out=moe[:, t, :], in0=last_tiles[k * PAIRS + t],
                        scalar=gates[:, e, t:t + 1], in1=moe[:, t, :], op0=ALU.mult, op1=ALU.add)\
                        .then_inc(S["next_to_last_added" if k == 0 else "result_ready"], 1)


_INS = ["x", "ctx_1024", "g_xattn", "g_ffn", "L0_xattn_w_q", "L0_xattn_w_k", "L0_xattn_w_v",
        "L0_xattn_w_o", "L0_ffn_router_w", "L0_ffn_rms_w", "L0_ffn_w1", "L0_ffn_w2",
        "L0_ffn_rms_w_s", "L0_ffn_w1_s", "L0_ffn_w2_s"]


def kernel(**inputs):
    import numpy as _np
    import concourse.bacc as _bacc
    from concourse import mybir as _mybir
    from concourse.bass_utils import run_bass_kernel_spmd as _run

    nc = _bacc.Bacc("TRN2", target_bir_lowering=False, num_devices=1)
    arrays, args = {}, {}
    for name in _INS:
        a = _np.ascontiguousarray(inputs[name])
        arrays[f"in_{name}_dram"] = a
        args[name] = nc.dram_tensor(f"in_{name}_dram", a.shape, _mybir.dt.from_np(a.dtype),
                                    kind="ExternalInput").ap()
    out = nc.dram_tensor("out_0_dram", (B, Q, D), _mybir.dt.float32, kind="ExternalOutput").ap()
    build(nc, args, out)
    r = _run(nc, [arrays], core_ids=[0])
    return r.results[0]["out_0_dram"]
```
